# Optimizing a Trainium2 kernel written in Bass

```python
import numpy as np
import jax
import jax.numpy as jnp

def _softmax(x, axis=-1):
    return jax.nn.softmax(x, axis=axis)

def _gelu(x):
    return jax.nn.gelu(x, approximate=True)

def _silu(x):
    return jax.nn.silu(x)

def _sigmoid(x):
    return jax.nn.sigmoid(x)

def _layernorm(x, axis=-1, eps=1e-05):
    m = jnp.mean(x, axis=axis, keepdims=True)
    v = jnp.var(x, axis=axis, keepdims=True)
    return (x - m) / jnp.sqrt(v + eps)

def _scatter_add(tgt, idx, src, axis=0):
    return tgt.at[idx].add(src)

def _segment_sum(src, seg, n):
    return jax.ops.segment_sum(src, seg, n)
kernel_name = 'mk_decoder_postln_d1_seqx_r8_61fc00'

def setup_inputs(seed: int=0):
    np.random.seed(seed)
    _w = jnp.asarray

    def _rec_inputs():
        import jax
        import jax.numpy as jnp
        _rk = jax.random.key(seed)
        x = 2.818e-05 + 1 * jax.random.normal(jax.random.fold_in(_rk, 1), (4, 256, 256), jnp.float32)
        _lenS = 256 - jax.random.randint(jax.random.fold_in(_rk, 7), (4,), 0, max(1, 256 // 4) + 1, jnp.int32)
        _lenS2 = 256 - jax.random.randint(jax.random.fold_in(_rk, 8), (4,), 0, max(1, 256 // 4) + 1, jnp.int32)
        _ctx_1024P = jax.random.normal(jax.random.fold_in(_rk, 11), (4, 16, 128), jnp.float32)
        _ctx_1024c = jax.random.dirichlet(jax.random.fold_in(_rk, 511), 0.3 * jnp.ones((16,), jnp.float32), (4, 256))
        _ctx_1024t = jnp.einsum('bsk,bkd->bsd', _ctx_1024c, _ctx_1024P)
        _ctx_1024t = _ctx_1024t * jax.lax.rsqrt(jnp.mean(jnp.square(_ctx_1024t)) + 1e-12) * 0.953939
        ctx_1024 = 7.22013e-05 + 1.00017 * (_ctx_1024t + 0.3 * jax.random.normal(jax.random.fold_in(_rk, 611), (4, 256, 128), jnp.float32))
        return (x, ctx_1024)
    x, ctx_1024 = _rec_inputs()

    def _L0_attn_setup():
        import jax, jax.numpy as jnp
        import numpy as np
        B, S, HID = (1, 512, 256)
        NH, NKV, D = (16, 4, 128)
        QPG = NH // NKV
        GROUP = (QPG + 2) * D
        TOTAL = NKV * GROUP
        key = jax.random.key(seed)
        k0, k1, k2 = jax.random.split(key, 3)
        x = jax.random.normal(k0, (B, S, HID), dtype=jnp.float32)
        weight_qkv = jax.random.normal(k1, (TOTAL, HID), dtype=jnp.float32) * 0.02
        weight_proj = jax.random.normal(k2, (HID, NH * D), dtype=jnp.float32) * 0.02
        return {'x': x, 'weight_qkv': weight_qkv, 'weight_proj': weight_proj}
    _L0_attn_all = _L0_attn_setup()
    _L0_attn_in = {k: v for k, v in _L0_attn_all.items() if k in ('weight_qkv', 'weight_proj')}
    del _L0_attn_all

    def _L0_xattn_setup():
        import jax, jax.numpy as jnp
        import numpy as np
        B_, L_, D_MODEL = (4, 256, 128)
        D_STATE, D_CONV, EXPAND = (16, 4, 2)
        D_INNER = EXPAND * D_MODEL
        DT_RANK = (D_MODEL + 15) // 16

        def silu(x):
            return x * jax.nn.sigmoid(x)
        key = jax.random.key(seed)
        ks = jax.random.split(key, 10)
        f32 = jnp.float32
        hidden_states = jax.random.normal(ks[0], (B_, L_, D_MODEL), dtype=f32)
        z = jax.random.normal(ks[1], (B_, D_INNER, L_), dtype=f32)
        in_proj_w = jax.random.normal(ks[2], (D_INNER, D_MODEL), dtype=f32) * 0.02
        conv_w = jax.random.normal(ks[3], (D_INNER, 1, D_CONV), dtype=f32) * 0.1
        conv_b = jax.random.normal(ks[4], (D_INNER,), dtype=f32) * 0.02
        x_proj_w = jax.random.normal(ks[5], (DT_RANK + 2 * D_STATE, D_INNER), dtype=f32) * 0.02
        dt_proj_w = jax.random.uniform(ks[6], (D_INNER, DT_RANK), dtype=f32, minval=-DT_RANK ** (-0.5), maxval=DT_RANK ** (-0.5))
        dt = jnp.exp(jax.random.uniform(ks[7], (D_INNER,), dtype=f32, minval=np.log(0.001), maxval=np.log(0.1)))
        dt_proj_b = jnp.log(jnp.expm1(dt))
        A_log = jnp.log(jnp.broadcast_to(jnp.arange(1, D_STATE + 1, dtype=f32), (D_INNER, D_STATE)))
        D = jnp.ones((D_INNER,), f32)
        return {'hidden_states': hidden_states, 'z': z, 'in_proj_w': in_proj_w, 'conv_w': conv_w, 'conv_b': conv_b, 'x_proj_w': x_proj_w, 'dt_proj_w': dt_proj_w, 'dt_proj_b': dt_proj_b, 'A_log': A_log, 'D': D}
    _L0_xattn_all = _L0_xattn_setup()
    _L0_xattn_in = {k: v for k, v in _L0_xattn_all.items() if k in ('in_proj_w', 'conv_w', 'conv_b', 'x_proj_w', 'dt_proj_w', 'dt_proj_b', 'A_log', 'D')}
    del _L0_xattn_all

    def _L0_ffn_setup():
        import jax, jax.numpy as jnp
        import numpy as np
        DIM = 256
        N_EXPERTS = 8
        TOP_K = 2
        key = jax.random.key(seed)
        ks = jax.random.split(key, 5)
        x = jax.random.normal(ks[0], (4, 512, DIM), dtype=jnp.float32)
        W_up = jax.random.normal(ks[1], (DIM, DIM), dtype=jnp.float32) * (1.0 / np.sqrt(DIM))
        W_down = jax.random.normal(ks[2], (DIM, DIM), dtype=jnp.float32) * (1.0 / np.sqrt(DIM))
        W_gate = jax.random.normal(ks[3], (N_EXPERTS, DIM), dtype=jnp.float32) * (1.0 / np.sqrt(DIM))
        W_expert = jax.random.normal(ks[4], (DIM, DIM), dtype=jnp.float32) * (1.0 / np.sqrt(DIM))
        return {'x': x, 'W_up': W_up, 'W_down': W_down, 'W_gate': W_gate, 'W_expert': W_expert}
    _L0_ffn_all = _L0_ffn_setup()
    _L0_ffn_in = {k: v for k, v in _L0_ffn_all.items() if k in ('W_up', 'W_down', 'W_gate', 'W_expert')}
    del _L0_ffn_all
    return {'x': x, 'ctx_1024': ctx_1024, 'L0_attn_weight_qkv': _L0_attn_in['weight_qkv'], 'L0_attn_weight_proj': _L0_attn_in['weight_proj'], 'L0_xattn_in_proj_w': _L0_xattn_in['in_proj_w'], 'L0_xattn_conv_w': _L0_xattn_in['conv_w'], 'L0_xattn_conv_b': _L0_xattn_in['conv_b'], 'L0_xattn_x_proj_w': _L0_xattn_in['x_proj_w'], 'L0_xattn_dt_proj_w': _L0_xattn_in['dt_proj_w'], 'L0_xattn_dt_proj_b': _L0_xattn_in['dt_proj_b'], 'L0_xattn_A_log': _L0_xattn_in['A_log'], 'L0_xattn_D': _L0_xattn_in['D'], 'L0_ffn_W_up': _L0_ffn_in['W_up'], 'L0_ffn_W_down': _L0_ffn_in['W_down'], 'L0_ffn_W_gate': _L0_ffn_in['W_gate'], 'L0_ffn_W_expert': _L0_ffn_in['W_expert']}

def reference(x, ctx_1024, L0_attn_weight_qkv, L0_attn_weight_proj, L0_xattn_in_proj_w, L0_xattn_conv_w, L0_xattn_conv_b, L0_xattn_x_proj_w, L0_xattn_dt_proj_w, L0_xattn_dt_proj_b, L0_xattn_A_log, L0_xattn_D, L0_ffn_W_up, L0_ffn_W_down, L0_ffn_W_gate, L0_ffn_W_expert):
    import jax
    import jax.numpy as jnp

    def _L0_attn_ref(x, weight_qkv, weight_proj):
        import jax, jax.numpy as jnp
        import numpy as np
        B, S, HID = (1, 512, 256)
        NH, NKV, D = (16, 4, 128)
        QPG = NH // NKV
        GROUP = (QPG + 2) * D
        TOTAL = NKV * GROUP
        b, s, _ = x.shape
        qkv = jnp.einsum('bsh,ph->bsp', x, weight_qkv).reshape(b, s, NKV, GROUP)
        q = qkv[..., :QPG * D].reshape(b, s, NKV, QPG, D)
        k = qkv[..., QPG * D:(QPG + 1) * D]
        v = qkv[..., (QPG + 1) * D:]
        scale = 1.0 / jnp.sqrt(jnp.float32(D))
        scores = jnp.einsum('bsgqd,btgd->bgqst', q, k) * scale
        causal = jnp.tril(jnp.ones((s, s), dtype=bool))
        scores = jnp.where(causal, scores, jnp.finfo(scores.dtype).min)
        attn = jax.nn.softmax(scores, axis=-1)
        out = jnp.einsum('bgqst,btgd->bsgqd', attn, v)
        out = out.reshape(b, s, NH * D)
        return jnp.einsum('bse,he->bsh', out, weight_proj)

    def _L0_xattn_ref(hidden_states, z, in_proj_w, conv_w, conv_b, x_proj_w, dt_proj_w, dt_proj_b, A_log, D):
        import jax, jax.numpy as jnp
        import numpy as np
        B_, L_, D_MODEL = (4, 256, 128)
        D_STATE, D_CONV, EXPAND = (16, 4, 2)
        D_INNER = EXPAND * D_MODEL
        DT_RANK = (D_MODEL + 15) // 16

        def silu(x):
            return x * jax.nn.sigmoid(x)
        Bsz, L, _ = hidden_states.shape
        d_inner, _, d_conv = conv_w.shape
        dt_rank = dt_proj_w.shape[1]
        d_state = A_log.shape[1]
        x = jnp.einsum('bld,ed->bel', hidden_states, in_proj_w)
        xc = jax.lax.conv_general_dilated(x, conv_w, window_strides=(1,), padding=[(d_conv - 1, 0)], feature_group_count=d_inner, dimension_numbers=('NCH', 'OIH', 'NCH'))
        x = silu(xc + conv_b[None, :, None])
        x_dbl = jnp.einsum('bdl,ed->bel', x, x_proj_w)
        dt_low, Bm, Cm = jnp.split(x_dbl, [dt_rank, dt_rank + d_state], axis=1)
        dt = jnp.einsum('brl,dr->bdl', dt_low, dt_proj_w)
        dt = jax.nn.softplus(dt + dt_proj_b[None, :, None])
        A = -jnp.exp(A_log)
        dt_t = jnp.moveaxis(dt, -1, 0)
        B_t = jnp.moveaxis(Bm, -1, 0)
        C_t = jnp.moveaxis(Cm, -1, 0)
        u_t = jnp.moveaxis(x, -1, 0)

        def step(state, inp):
            d, b, c, u = inp
            dA = jnp.exp(d[..., None] * A)
            state = state * dA + (d * u)[..., None] * b[:, None, :]
            y = jnp.einsum('bdn,bn->bd', state, c)
            return (state, y)
        state0 = jnp.zeros((Bsz, d_inner, d_state), x.dtype)
        _, ys = jax.lax.scan(step, state0, (dt_t, B_t, C_t, u_t))
        y = jnp.moveaxis(ys, 0, 2)
        y = y + D[None, :, None] * x
        y = y * silu(z)
        return jnp.swapaxes(y, 1, 2)

    def _L0_ffn_ref(x, W_up, W_down, W_gate, W_expert):
        import jax, jax.numpy as jnp
        import numpy as np
        DIM = 256
        N_EXPERTS = 8
        TOP_K = 2
        logits = jnp.einsum('bsd,ed->bse', x, W_gate)
        routing_weights, selected_experts = jax.lax.top_k(logits, TOP_K)
        shared_out = jnp.einsum('bsd,od->bso', jax.nn.relu(jnp.einsum('bsd,od->bso', x, W_up)), W_down)
        rw = jax.nn.softmax(routing_weights, axis=-1)
        expert_out = jnp.einsum('bsd,do->bso', x, W_expert)
        moe_out = jnp.sum(rw, axis=-1, keepdims=True) * expert_out
        return shared_out + moe_out
    x = _layernorm(x + _L0_attn_ref(x, L0_attn_weight_qkv, L0_attn_weight_proj), axis=-1)
    x = _layernorm(x + _L0_xattn_ref(ctx_1024, x, L0_xattn_in_proj_w, L0_xattn_conv_w, L0_xattn_conv_b, L0_xattn_x_proj_w, L0_xattn_dt_proj_w, L0_xattn_dt_proj_b, L0_xattn_A_log, L0_xattn_D), axis=-1)
    x = _layernorm(x + _L0_ffn_ref(x, L0_ffn_W_up, L0_ffn_W_down, L0_ffn_W_gate, L0_ffn_W_expert), axis=-1)
    return x

_drawn_inputs = setup_inputs


def setup_inputs(seed=0):
    import zlib

    import numpy as np

    out = dict(_drawn_inputs(seed))
    spreads = {'L0_xattn_D': (1.0, 0.6)}
    factors = {'ctx_1024': 4.444,
     'L0_xattn_in_proj_w': 4.447,
     'L0_xattn_conv_w': 4.646,
     'L0_xattn_conv_b': 8.0,
     'L0_xattn_x_proj_w': 8.0,
     'L0_xattn_dt_proj_w': 8.0,
     'L0_xattn_dt_proj_b': 8.0,
     'L0_xattn_A_log': 8.0,
     'L0_ffn_W_gate': 8.0}
    for name, (base, spread) in spreads.items():
        noise = np.random.default_rng([zlib.crc32(name.encode()), seed]).standard_normal(out[name].shape)
        drawn = base * np.exp(spread * noise) if base else spread * noise
        out[name] = jnp.asarray(drawn.astype(out[name].dtype))
    for name, factor in factors.items():
        out[name] = (out[name] * factor).astype(out[name].dtype)
    return out
```

```python
from contextlib import ExitStack

import concourse.bass as bass
from concourse import mybir

ALU = mybir.AluOpType
ACT = mybir.ActivationFunctionType
AX = mybir.AxisListType
F32 = mybir.dt.float32
F16 = mybir.dt.float16
BF16 = mybir.dt.bfloat16
I32 = mybir.dt.int32

P = 128
B, S, HID = 4, 256, 256
NH, NKV, D = 16, 4, 128
QPG = NH // NKV
GW = (QPG + 2) * D
NG = B * NKV
T = B * S
KT = HID // P
DM, NS, DC, DTR = 128, 16, 4, 8
DT = 256 // P
NE = 8
EPS = 1e-5

W_SCALE = 64.0
QKV_OUT = 1.0 / 16.0
SCORE_SCALE = 1.0 / 16.0 / float(D) ** 0.5
P_SCALE = 4096.0
O_OUT = 1.0 / 4096.0
Y_OUT = 1.0 / 256.0
MASKED = -3.0e38
SMALL = 0.03


def decoder_kernel(nc, xT, x, wqkvT, wpT, ctxT, inT, conv_w, conv_b, xprojT, dtT, dt_b, A_log, D_skip,
                   upT, downT, gateT, expert, out):
    bc_rows = nc.dram_tensor("bc_rows", (2 * NS, T), F32, kind="Internal").ap()
    with ExitStack() as ctx:
        def sb(name, shape, dt=F32):
            return ctx.enter_context(nc.sbuf_tensor(name, shape, dt))

        def sem(name):
            return ctx.enter_context(nc.semaphore(name))

        xT_f = sb("xT_f", [P, KT, T])
        xT_hi = sb("xT_hi", [P, KT, T], F16)
        xT_lo = sb("xT_lo", [P, KT, T], F16)
        wqkv_f = sb("wqkv_f", [P, KT, NKV * GW])
        wqkv_hi = sb("wqkv_hi", [P, KT, NKV * GW], F16)
        wqkv_lo = sb("wqkv_lo", [P, KT, NKV * GW], F16)
        wp_f = sb("wp_f", [P, NH, HID])
        wp_hi = sb("wp_hi", [P, NH, HID], F16)
        wp_lo = sb("wp_lo", [P, NH, HID], F16)
        resid = sb("resid", [P, B * KT, HID])
        q_hi = sb("q_hi", [P, QPG * S], F16)
        q_lo = sb("q_lo", [P, QPG * S], F16)
        k_hi = sb("k_hi", [P, S], F16)
        k_lo = sb("k_lo", [P, S], F16)
        v_hi = sb("v_hi", [P, 2, D], F16)
        v_lo = sb("v_lo", [P, 2, D], F16)
        e_sb = sb("e_sb", [P, QPG, 3 * P])
        pt_hi = sb("pt_hi", [P, 2, 3 * P], F16)
        pt_lo = sb("pt_lo", [P, 2, 3 * P], F16)
        o_hi = sb("o_hi", [P, QPG, S], F16)
        o_lo = sb("o_lo", [P, QPG, S], F16)
        negmax = sb("negmax", [P, 2 * QPG])
        ebias = sb("ebias", [P, 2 * QPG])
        esum = sb("esum", [P, QPG, 2])
        rsum = sb("rsum", [P, QPG, 2])
        ident = sb("ident", [P, P])
        ident_b = sb("ident_b", [P, P], BF16)
        mask_f = sb("mask_f", [P, P])
        mask_b = sb("mask_b", [P, P], BF16)
        in_w = sb("in_w", [P, 2 * P])
        cw = sb("cw", [P, DT, DC])
        cb = sb("cb", [P, DT])
        xp_w = sb("xp_w", [P, DT, DTR + 2 * NS])
        dt_w = sb("dt_w", [DTR, 2 * P])
        dtb = sb("dtb", [P, DT])
        a_mat = sb("a_mat", [P, DT, NS])
        d_col = sb("d_col", [P, DT])
        u = sb("u", [P, DT, T])
        dt = sb("dt", [P, DT, T])
        du = sb("du", [P, DT, T])
        y_acc = sb("y_acc", [P, DT, T])
        decay = sb("decay", [P, DT, T])
        drive = sb("drive", [P, DT, T])
        h_st = sb("h_st", [P, DT, B * (S + DC - 1)])
        b_row = sb("b_row", [P, T])
        c_row = sb("c_row", [P, T])
        xdbl = sb("xdbl", [DTR + 2 * NS, T])
        up_w = sb("up_w", [P, KT, HID])
        down_w = sb("down_w", [P, KT, HID])
        gate_w = sb("gate_w", [P, KT, NE])
        exp_w = sb("exp_w", [P, KT, HID])
        stats = sb("stats", [P, 2 * B, 6])
        mv = sb("mv", [P, 2 * B, 2])
        veps = sb("veps", [P, 2 * B])
        rstd = sb("rstd", [P, 2 * B])
        mhalf = sb("mhalf", [P, 2 * B])
        top = sb("top", [P, 2 * B, 8])
        top_d = sb("top_d", [P, 2 * B, 2])
        top_e = sb("top_e", [P, 2 * B, 2])
        top_s = sb("top_s", [P, 2 * B, 1])
        top_r = sb("top_r", [P, 2 * B, 1])
        rw = sb("rw", [P, 2 * B, 2])
        rw_sum = sb("rw_sum", [P, 2 * B, 1])

        ctx_sb = du[:, 0, :]
        x_pad = h_st[:].rearrange("p j (b l) -> p j b l", b=B)
        wq_flat = wqkv_f[:].rearrange("p k n -> p (k n)")
        z_silu = wq_flat[:, 0:2048].rearrange("p (t n) -> p t n", n=HID)
        gated = wq_flat[:, 2048:4096].rearrange("p (t n) -> p t n", n=HID)
        x2T = wq_flat[:, 4096:6144].rearrange("p (k t) -> p k t", k=KT)
        wp_flat = wp_f[:].rearrange("p h n -> p (h n)")
        hidden = wp_flat[:, 0:2048].rearrange("p (k t) -> p k t", k=KT)
        res3 = wp_flat[:, 2048:4096].rearrange("p (t n) -> p t n", n=HID)
        res2 = y_acc[:].rearrange("p j (t n) -> p (j t) n", n=HID)

        bank = [ctx.enter_context(nc.psum_tensor(f"bank{n}", [P, 512], F32)) for n in range(8)]
        ps_s0 = bank[0][:].rearrange("p (h t) -> p h t", h=QPG)
        ps_s1 = [bank[1 + n][:].rearrange("p (h t) -> p h t", h=2) for n in range(2)]
        ps_qkv, ps_proj, ps_o = bank[3], bank[4], bank[7]
        ps_pt = [bank[5], bank[6]]

        x_loaded, wq0_loaded, wq_loaded, wp_loaded = sem("x_loaded"), sem("wq0_loaded"), sem("wq_loaded"), sem("wp_loaded")
        ctx_loaded, scanw_loaded, late_loaded = sem("ctx_loaded"), sem("scanw_loaded"), sem("late_loaded")
        bc_stored, b_loaded, c_loaded, out_stored = sem("bc_stored"), sem("b_loaded"), sem("c_loaded"), sem("out_stored")
        zeroed, consts = sem("zeroed"), sem("consts")
        x_hi_done, x_lo_done = sem("x_hi_done"), sem("x_lo_done")
        wq_hi_done, wq_lo_done = sem("wq_hi_done"), sem("wq_lo_done")
        wp_hi_done, wp_lo_done = sem("wp_hi_done"), sem("wp_lo_done")
        in_done, pad_done, conv_done, u_done = sem("in_done"), sem("pad_done"), sem("conv_done"), sem("u_done")
        xp_done, xdbl_done, dtp_done = sem("xp_done"), sem("xdbl_done"), sem("dtp_done")
        sp_abs, sp_exp, sp_ln, sp_dve, a_exp, a_done = (sem("sp_abs"), sem("sp_exp"), sem("sp_ln"), sem("sp_dve"),
                                                        sem("a_exp"), sem("a_done"))
        du_done, yinit_done = sem("du_done"), sem("yinit_done")
        qkv_ready, qkv_hi, qkv_lo = sem("qkv_ready"), sem("qkv_hi"), sem("qkv_lo")
        scores_ready, max_done, bias_ready, exp_done = sem("scores_ready"), sem("max_done"), sem("bias_ready"), sem("exp_done")
        rsum_ready, probs_ready = sem("rsum_ready"), sem("probs_ready")
        pt_ready, pt_hi_done, pt_lo_done = sem("pt_ready"), sem("pt_hi_done"), sem("pt_lo_done")
        pv_done, o_hi_done, o_lo_done = sem("pv_done"), sem("o_hi_done"), sem("o_lo_done")
        proj_done, proj_added = sem("proj_done"), sem("proj_added")
        pool_turn = sem("pool_turn")
        decay_ready, drive_ready, scan_done, hc_ready, acc_done = (sem("decay_ready"), sem("drive_ready"), sem("scan_done"),
                                                                   sem("hc_ready"), sem("acc_done"))
        st_done, mv_done, veps_done, rstd_done = sem("st_done"), sem("mv_done"), sem("veps_done"), sem("rstd_done")
        x1_ready, z_ready, gated_ready, gT_ready, res2_ready = (sem("x1_ready"), sem("z_ready"), sem("gated_ready"),
                                                                sem("gT_ready"), sem("res2_ready"))
        x2_ready, x2T_ps, x2T_ready = sem("x2_ready"), sem("x2T_ps"), sem("x2T_ready")
        up_done, relu_done, gates_done, moe_done = sem("up_done"), sem("relu_done"), sem("gates_done"), sem("moe_done")
        route, route_exp, mix_done, res3_ready, y_ready = (sem("route"), sem("route_exp"), sem("mix_done"),
                                                           sem("res3_ready"), sem("y_ready"))

        block = ctx.enter_context(nc.Block())

        @block.sync
        def _(sp):
            sp.dma_start(ctx_sb, ctxT).then_inc(ctx_loaded, 16)
            sp.dma_start(in_w[:], inT).then_inc(ctx_loaded, 16)
            sp.dma_start(xT_f[:], xT.rearrange("(k p) t -> p k t", p=P)).then_inc(x_loaded, 16)
            wq_v = wqkvT.rearrange("(k p) n -> p k n", p=P)
            sp.dma_start(wqkv_f[:, :, 0:GW], wq_v[:, :, 0:GW]).then_inc(wq0_loaded, 16)
            sp.dma_start(cw[:], conv_w.rearrange("(j p) k -> p j k", p=P)).then_inc(scanw_loaded, 16)
            sp.dma_start(xp_w[:], xprojT.rearrange("(j p) n -> p j n", p=P)).then_inc(scanw_loaded, 16)
            sp.dma_start(dt_w[:], dtT).then_inc(scanw_loaded, 16)
            sp.dma_start(a_mat[:], A_log.rearrange("(j p) n -> p j n", p=P)).then_inc(scanw_loaded, 16)
            with nc.allow_non_contiguous_dma(reason="three short columns"):
                sp.dma_start(cb[:], conv_b.rearrange("(j p) -> p j", p=P)).then_inc(scanw_loaded, 16)
                sp.dma_start(dtb[:], dt_b.rearrange("(j p) -> p j", p=P)).then_inc(scanw_loaded, 16)
                sp.dma_start(d_col[:], D_skip.rearrange("(j p) -> p j", p=P)).then_inc(scanw_loaded, 16)
            sp.dma_start(wqkv_f[:, :, GW:], wq_v[:, :, GW:]).then_inc(wq_loaded, 16)
            sp.dma_start(wp_f[:], wpT.rearrange("(h p) n -> p h n", p=P)).then_inc(wp_loaded, 16)
            sp.dma_start(resid[:], x.rearrange("(t p) n -> p t n", p=P)).then_inc(late_loaded, 16)
            sp.dma_start(up_w[:], upT.rearrange("(k p) n -> p k n", p=P)).then_inc(late_loaded, 16)
            sp.dma_start(down_w[:], downT.rearrange("(k p) n -> p k n", p=P)).then_inc(late_loaded, 16)
            sp.dma_start(gate_w[:], gateT.rearrange("(k p) n -> p k n", p=P)).then_inc(late_loaded, 16)
            sp.dma_start(exp_w[:], expert.rearrange("(k p) n -> p k n", p=P)).then_inc(late_loaded, 16)
            sp.wait_ge(xdbl_done, 2)
            sp.dma_start(bc_rows, xdbl[DTR:, :]).then_inc(bc_stored, 16)
            sp.wait_ge(bc_stored, 16)
            sp.dma_start(b_row[:], bc_rows[0:1, :].broadcast_to((P, T))).then_inc(b_loaded, 16)
            sp.dma_start(c_row[:], bc_rows[NS:NS + 1, :].broadcast_to((P, T))).then_inc(c_loaded, 16)
            with sp.Fori(1, NS) as n:
                sp.wait_ge(drive_ready, 2 * n)
                sp.dma_start(b_row[:], bc_rows[bass.ds(n, 1), :].broadcast_to((P, T))).then_inc(b_loaded, 16)
                sp.wait_ge(hc_ready, 2 * n)
                sp.dma_start(c_row[:], bc_rows[bass.ds(n + NS, 1), :].broadcast_to((P, T))).then_inc(c_loaded, 16)
            out_v = out.rearrange("b (a p) n -> b p a n", p=P)
            for b in range(B):
                sp.wait_ge(y_ready, 2 * b + 2)
                sp.dma_start(out_v[b], res3[:, 2 * b:2 * b + 2, :]).then_inc(out_stored, 16)
            sp.wait_ge(out_stored, 16 * B)

        @block.tensor
        def _(pe):
            def products(o, lhs, rhs, start=True, stop=True, skip=False):
                n = len(lhs)
                for k in range(n):
                    (lh, ll), (rh, rl) = lhs[k], rhs[k]
                    pe.matmul(o, lh, rh, start=start and k == 0, stop=False, skip_group_check=skip)
                    pe.matmul(o, lh, rl, start=False, stop=False, skip_group_check=skip)
                    m = pe.matmul(o, ll, rh, start=False, stop=stop and k == n - 1, skip_group_check=skip)
                return m

            def wq(g, off):
                return [(wqkv_hi[:, k, bass.ds(g * GW + off, D)], wqkv_lo[:, k, bass.ds(g * GW + off, D)]) for k in range(KT)]

            def xt(at, n):
                return [(xT_hi[:, k, bass.ds(at, n)], xT_lo[:, k, bass.ds(at, n)]) for k in range(KT)]

            def bank_free(i, unit):
                pe.wait_ge(qkv_lo, 4 * i + unit)

            def q_unit(i, b, g, pair):
                for n in range(2):
                    m = products(ps_qkv[:, n * S:(n + 1) * S], wq(g, (2 * pair + n) * D), xt(b * S, S))
                m.then_inc(qkv_ready, 1)

            def k_unit(i, b, g):
                products(ps_qkv[:, 0:S], wq(g, QPG * D), xt(b * S, S)).then_inc(qkv_ready, 1)

            def v_unit(i, b, g):
                for t in range(2):
                    m = products(ps_qkv[:, t * D:(t + 1) * D], xt(b * S + t * P, P), wq(g, (QPG + 1) * D))
                m.then_inc(qkv_ready, 1)

            def scores_rows0(i):
                pe.matmul(ps_s0, ident_b[:], mask_b[:].unsqueeze(1).broadcast_to((P, QPG, P)),
                          start=True, stop=False, skip_group_check=True)
                for h in range(QPG):
                    m = products(ps_s0[:, h, :], [(q_hi[:, h * S:h * S + P], q_lo[:, h * S:h * S + P])],
                                 [(k_hi[:, 0:P], k_lo[:, 0:P])], start=False, skip=True)
                m.then_inc(scores_ready, 1)

            def scores_rows1(i, pair):
                o = ps_s1[pair]
                pe.matmul(o[:, :, P:S], ident_b[:], mask_b[:].unsqueeze(1).broadcast_to((P, 2, P)),
                          start=True, stop=False, skip_group_check=True)
                for n in range(2):
                    q0 = (2 * pair + n) * S + P
                    m = products(o[:, n, :], [(q_hi[:, q0:q0 + P], q_lo[:, q0:q0 + P])], [(k_hi[:], k_lo[:])],
                                 start=False, skip=True)
                m.then_inc(scores_ready, 1)

            def transposes(i, h):
                k = 4 * i + h
                pe.wait_ge(probs_ready, k + 1)
                if not (isinstance(k, int) and k < 2):
                    pe.wait_ge(pt_lo_done, k - 1)
                o = ps_pt[h % 2]
                pe.transpose(o[:, 0:P], e_sb[:, h, 0:P], ident[:])
                pe.transpose(o[:, P:2 * P], e_sb[:, h, P:2 * P], ident[:])
                pe.transpose(o[:, 2 * P:3 * P], e_sb[:, h, 2 * P:3 * P], ident[:]).then_inc(pt_ready, 1)

            def pv(i, h):
                k = 4 * i + h
                pe.wait_ge(pt_lo_done, k + 1)
                if h % 2 == 0 and not (isinstance(k, int) and k == 0):
                    pe.wait_ge(o_lo_done, 2 * i + h // 2)
                o = ps_o[:, (h % 2) * S:(h % 2 + 1) * S]
                ph, pl = pt_hi[:, h % 2, :], pt_lo[:, h % 2, :]
                products(o, [(v_hi[:, 0, :], v_lo[:, 0, :])], [(ph[:, 0:S], pl[:, 0:S])], stop=False, skip=True)
                products(o[:, P:S], [(v_hi[:, 1, :], v_lo[:, 1, :])], [(ph[:, S:S + P], pl[:, S:S + P])],
                         start=False, skip=True).then_inc(pv_done, 1)

            def project(i, g, pair):
                pe.wait_ge(o_lo_done, 2 * i + pair + 1)
                if pair == 0 and not (isinstance(i, int) and i == 0):
                    pe.wait_ge(proj_added, i)
                for n in range(2):
                    h = 2 * pair + n
                    for a in range(2):
                        m = products(ps_proj[:, a * HID:(a + 1) * HID],
                                     [(o_hi[:, h, a * P:(a + 1) * P], o_lo[:, h, a * P:(a + 1) * P])],
                                     [(wp_hi[:, bass.ds(g * QPG + h, 1), :].rearrange("p a n -> p (a n)"),
                                       wp_lo[:, bass.ds(g * QPG + h, 1), :].rearrange("p a n -> p (a n)"))],
                                     start=(h == 0 and a == 0), stop=(h == QPG - 1), skip=True)
                m.then_inc(proj_done, 1)

            pe.wait_ge(ctx_loaded, 32)
            for j in range(DT):
                for c in range(2):
                    pe.matmul(bank[2 * j + c][:], in_w[:, j * P:(j + 1) * P], ctx_sb[:, c * 512:(c + 1) * 512],
                              start=True, stop=True).then_inc(in_done, 1)
            pe.wait_ge(scanw_loaded, 16 * 7)
            pe.wait_ge(u_done, 2)
            for c in range(2):
                for j in range(DT):
                    m = pe.matmul(bank[c][0:DTR + 2 * NS, :], xp_w[:, j, :], u[:, j, c * 512:(c + 1) * 512],
                                  start=j == 0, stop=j == DT - 1)
                m.then_inc(xp_done, 1)
            pe.wait_ge(xdbl_done, 2)
            for j in range(DT):
                for c in range(2):
                    m = pe.matmul(bank[4 + 2 * j + c][:], dt_w[:, j * P:(j + 1) * P], xdbl[0:DTR, c * 512:(c + 1) * 512],
                                  start=True, stop=True)
                m.then_inc(dtp_done, 1)
            pe.wait_ge(consts, 4)
            pe.wait_ge(x_lo_done, 1)
            pe.wait_ge(wq_lo_done, 4)
            pe.wait_ge(wp_lo_done, 1)
            pe.wait_ge(sp_dve, 2 * 6)
            q_unit(0, 0, 0, 0)
            bank_free(0, 1)
            q_unit(0, 0, 0, 1)
            bank_free(0, 2)
            k_unit(0, 0, 0)
            bank_free(0, 3)
            v_unit(0, 0, 0)

            def step(i, first=False, last=False):
                nb, ng = ((i + 1) >> 2) & 3, (i + 1) & 3
                pe.wait_ge(qkv_lo, 4 * i + 3)
                if not first:
                    pe.wait_ge(exp_done, 4 * i)
                scores_rows0(i)
                scores_rows1(i, 0)
                scores_rows1(i, 1)
                bank_free(i, 4)
                if not last:
                    q_unit(i + 1, nb, ng, 0)
                if not first:
                    project(i - 1, (i - 1) & 3, 1)
                if not last:
                    bank_free(i + 1, 1)
                    q_unit(i + 1, nb, ng, 1)
                transposes(i, 0)
                transposes(i, 1)
                pv(i, 0)
                if not last:
                    bank_free(i + 1, 2)
                    k_unit(i + 1, nb, ng)
                pv(i, 1)
                transposes(i, 2)
                transposes(i, 3)
                project(i, i & 3, 0)
                pv(i, 2)
                pv(i, 3)
                if not last:
                    bank_free(i + 1, 3)
                    v_unit(i + 1, nb, ng)

            step(0, first=True)
            with pe.Fori(1, NG - 1) as i:
                step(i)
            step(NG - 1, last=True)
            project(NG - 1, NKV - 1, 1)

            pe.wait_ge(late_loaded, 16 * 5)
            for b in range(B):
                pe.wait_ge(gated_ready, b + 1)
                for a in range(2):
                    for j in range(2):
                        m = pe.transpose(bank[b][:, a * HID + j * P:a * HID + (j + 1) * P],
                                         gated[:, 2 * b + j, a * P:(a + 1) * P], ident[:])
                m.then_inc(gT_ready, 1)
            pe.wait_ge(proj_added, NG)
            for b in range(B):
                pe.wait_ge(x2_ready, 2 * b + 2)
                for k in range(KT):
                    for a in range(2):
                        m = pe.transpose(bank[4 + b][:, k * S + a * P:k * S + (a + 1) * P],
                                         res2[:, 2 * b + a, k * P:(k + 1) * P], ident[:])
                m.then_inc(x2T_ps, 1)
            for b in range(B):
                pe.wait_ge(x2T_ready, b + 1)
                for o in range(2):
                    for k in range(KT):
                        m = pe.matmul(bank[b][:, o * S:(o + 1) * S], up_w[:, k, o * P:(o + 1) * P],
                                      x2T[:, k, b * S:(b + 1) * S], start=k == 0, stop=k == KT - 1)
                m.then_inc(up_done, 1)
                for t in range(2 * b, 2 * b + 2):
                    for k in range(KT):
                        m = pe.matmul(bank[4][:, t * NE:(t + 1) * NE], x2T[:, k, t * P:(t + 1) * P], gate_w[:, k, :],
                                      start=k == 0, stop=k == KT - 1)
                m.then_inc(gates_done, 1)
            for t in range(2 * B):
                o = bank[(5, 6, 7, 0, 1, 2)[t % 6]]
                pe.wait_ge(relu_done, t // 2 + 1 if t < 6 else B)
                if t == 3:
                    pe.wait_ge(relu_done, 3)
                if t >= 6:
                    pe.wait_ge(mix_done, 2 * (t - 5))
                for k in range(KT):
                    pe.matmul(o[:, 0:HID], hidden[:, k, t * P:(t + 1) * P], down_w[:, k, :], start=k == 0, stop=k == KT - 1)
                for k in range(KT):
                    m = pe.matmul(o[:, HID:], x2T[:, k, t * P:(t + 1) * P], exp_w[:, k, :], start=k == 0, stop=k == KT - 1)
                m.then_inc(moe_done, 1)

        @block.scalar
        def _(act):
            act.wait_ge(x_loaded, 16)
            act.activation(xT_hi[:], xT_f[:], ACT.Copy).then_inc(x_hi_done, 1)
            act.wait_ge(wq0_loaded, 16)
            act.activation(wqkv_hi[:, :, 0:GW], wqkv_f[:, :, 0:GW], ACT.Copy, scale=W_SCALE).then_inc(wq_hi_done, 1)
            for j in range(DT):
                for c in range(2):
                    act.wait_ge(in_done, 2 * j + c + 1)
                    act.activation(x_pad[:, j, 2 * c:2 * c + 2, DC - 1:], bank[2 * j + c][:].rearrange("p (b l) -> p b l", b=2),
                                   ACT.Copy).then_inc(pad_done, 1)
            act.wait_ge(scanw_loaded, 16 * 7)
            for j in range(DT):
                act.wait_ge(conv_done, DC * (j + 1))
                act.activation(u[:, j, :], decay[:, j, :], ACT.Silu, bias=cb[:, j:j + 1]).then_inc(u_done, 1)
            for c in range(2):
                act.wait_ge(xp_done, c + 1)
                act.activation(xdbl[:, c * 512:(c + 1) * 512], bank[c][0:DTR + 2 * NS, :], ACT.Copy).then_inc(xdbl_done, 1)
            act.activation(a_mat[:], a_mat[:], ACT.Exp).then_inc(a_exp, 1)
            for j in range(DT):
                act.wait_ge(dtp_done, j + 1)
                for c in range(2):
                    act.activation(decay[:, j, c * 512:(c + 1) * 512], bank[4 + 2 * j + c][:], ACT.Abs,
                                   bias=dtb[:, j:j + 1]).then_inc(sp_abs, 1)
                act.wait_ge(sp_abs, 2 * j + 2)
                act.activation(decay[:, j, :], decay[:, j, :], ACT.Exp, scale=-1.0).then_inc(sp_exp, 1)
                act.wait_ge(sp_exp, j + 1)
                act.activation(dt[:, j, :], decay[:, j, :], ACT.Ln, bias=1.0).then_inc(sp_ln, 1)

            def qkv_high(i, unit):
                act.wait_ge(qkv_ready, 4 * i + unit + 1)
                o, n = ((q_hi[:, 0:512], 512), (q_hi[:, 512:1024], 512), (k_hi[:], 256),
                        (v_hi[:].rearrange("p t d -> p (t d)"), 256))[unit]
                act.activation(o, ps_qkv[:, 0:n], ACT.Copy, scale=QKV_OUT).then_inc(qkv_hi, 1)

            def scan_decay(i):
                for j in range(DT):
                    m = 2 * i + j
                    if not (isinstance(i, int) and i == 0):
                        act.wait_ge(scan_done, m - 1)
                    act.activation(decay[:, j, :].rearrange("p (b l) -> p b l", b=B)[:, :, 1:],
                                   dt[:, j, :].rearrange("p (b l) -> p b l", b=B)[:, :, 1:], ACT.Exp,
                                   scale=a_mat[:, j, bass.ds(i, 1)]).then_inc(decay_ready, 1)

            def exps(i, h, first):
                k = 4 * i + h
                act.wait_ge(bias_ready, 2 * i + (1 if h == 0 else 2))
                if not first:
                    act.wait_ge(pt_ready, k - 3)
                act.activation(e_sb[:, h, 0:P], ps_s0[:, h, :], ACT.Exp, bias=ebias[:, h:h + 1], scale=SCORE_SCALE,
                               accum_out=esum[:, h, 0:1])
                if h == 0:
                    act.wait_ge(bias_ready, 2 * i + 2)
                act.activation(e_sb[:, h, P:], ps_s1[h // 2][:, h % 2, :], ACT.Exp, bias=ebias[:, QPG + h:QPG + h + 1],
                               scale=SCORE_SCALE, accum_out=esum[:, h, 1:2]).then_inc(exp_done, 1)

            def pt_high(i, h):
                k = 4 * i + h
                act.wait_ge(pt_ready, k + 1)
                if not (isinstance(k, int) and k < 2):
                    act.wait_ge(pv_done, k - 1)
                act.activation(pt_hi[:, h % 2, :], ps_pt[h % 2][:, 0:3 * P], ACT.Copy).then_inc(pt_hi_done, 1)

            def o_high(i, pair):
                act.wait_ge(pv_done, 4 * i + 2 * pair + 2)
                if not (isinstance(i, int) and i == 0):
                    act.wait_ge(proj_done, 2 * i + pair - 1)
                act.activation(o_hi[:, 2 * pair:2 * pair + 2, :].rearrange("p h s -> p (h s)"), ps_o[:], ACT.Copy,
                               scale=O_OUT).then_inc(o_hi_done, 1)

            for unit in range(4):
                qkv_high(0, unit)
            act.wait_ge(a_done, 1)
            act.wait_ge(yinit_done, 2 + 8)

            def step(i, first=False, last=False):
                scan_decay(i)
                exps(i, 0, first)
                exps(i, 1, first)
                if not last:
                    qkv_high(i + 1, 0)
                exps(i, 2, first)
                exps(i, 3, first)
                if not last:
                    qkv_high(i + 1, 1)
                pt_high(i, 0)
                pt_high(i, 1)
                if not last:
                    qkv_high(i + 1, 2)
                o_high(i, 0)
                pt_high(i, 2)
                pt_high(i, 3)
                o_high(i, 1)
                if not last:
                    qkv_high(i + 1, 3)

            step(0, first=True)
            with act.Fori(1, NG - 1) as i:
                step(i)
            step(NG - 1, last=True)

            for b in range(B):
                act.wait_ge(x1_ready, 2 * b + 2)
                act.activation(z_silu[:, 2 * b:2 * b + 2, :], resid[:, 2 * b:2 * b + 2, :], ACT.Silu).then_inc(z_ready, 1)
            for b in range(B):
                act.wait_ge(x2T_ps, b + 1)
                act.activation(x2T[:, :, b * S:(b + 1) * S], bank[4 + b][:].rearrange("p (k s) -> p k s", k=KT),
                               ACT.Copy).then_inc(x2T_ready, 1)
            for b in range(B):
                act.wait_ge(up_done, b + 1)
                act.activation(hidden[:, :, b * S:(b + 1) * S], bank[b][:].rearrange("p (k s) -> p k s", k=KT),
                               ACT.Relu).then_inc(relu_done, 1)
            for b in range(B):
                act.wait_ge(route, 7 * b + 3)
                act.activation(top_e[:, 2 * b:2 * b + 2, :], top_d[:, 2 * b:2 * b + 2, :], ACT.Exp).then_inc(route_exp, 1)

        @block.vector
        def _(dve):
            dve.wait_ge(x_hi_done, 1)
            dve.tensor_tensor(xT_lo[:], xT_f[:], xT_hi[:], ALU.subtract).then_inc(x_lo_done, 1)

            def wq_low(g):
                dve.wait_ge(wq_hi_done, g + 1)
                w = slice(g * GW, (g + 1) * GW)
                dve.scalar_tensor_tensor(out=wqkv_lo[:, :, w], in0=wqkv_f[:, :, w], scalar=W_SCALE, in1=wqkv_hi[:, :, w],
                                         op0=ALU.mult, op1=ALU.subtract).then_inc(wq_lo_done, 1)

            wq_low(0)
            dve.wait_ge(scanw_loaded, 16 * 7)
            dve.wait_ge(zeroed, 1)
            for j in range(DT):
                dve.wait_ge(pad_done, 2 * (j + 1))
                acc = decay[:, j, :].rearrange("p (b l) -> p b l", b=B)
                dve.tensor_scalar(acc, x_pad[:, j, :, 0:S], cw[:, j, 0:1], None, ALU.mult).then_inc(conv_done, 1)
                for k in range(1, DC):
                    dve.wait_ge(conv_done, DC * j + k)
                    dve.scalar_tensor_tensor(out=acc, in0=x_pad[:, j, :, k:k + S], scalar=cw[:, j, k:k + 1], in1=acc,
                                             op0=ALU.mult, op1=ALU.add).then_inc(conv_done, 1)
            for g in range(1, NKV):
                wq_low(g)
            dve.wait_ge(a_exp, 1)
            dve.tensor_scalar(a_mat[:], a_mat[:], -1.0, None, ALU.mult).then_inc(a_done, 1)
            for j in range(DT):
                n = 6 * j
                e, r = decay[:, j, :], drive[:, j, :]
                dve.wait_ge(sp_exp, j + 1)
                for c in range(2):
                    m = dve.tensor_scalar(du[:, j, c * 512:(c + 1) * 512], bank[4 + 2 * j + c][:], dtb[:, j:j + 1], 0.0,
                                          ALU.add, ALU.max)
                m.then_inc(sp_dve, 1)
                dve.tensor_scalar(r, e, -0.25, None, ALU.mult).then_inc(sp_dve, 1)
                for s, c in enumerate((1.0 / 3.0, -0.5, 1.0)):
                    dve.wait_ge(sp_dve, n + 2 + s)
                    dve.scalar_tensor_tensor(out=r, in0=r, scalar=c, in1=e, op0=ALU.add, op1=ALU.mult).then_inc(sp_dve, 1)
                small = h_st[:, j, 0:T]
                dve.tensor_scalar(small, e, SMALL, None, ALU.is_lt).then_inc(sp_dve, 1)
                dve.wait_ge(sp_ln, j + 1)
                dve.wait_ge(sp_dve, n + 6)
                dve.copy_predicated(dt[:, j, :], small.bitcast(I32), r).then_inc(du_done, 1)
                dve.wait_ge(du_done, 3 * j + 1)
                dve.tensor_tensor(dt[:, j, :], dt[:, j, :], du[:, j, :], ALU.add).then_inc(du_done, 1)
                dve.wait_ge(du_done, 3 * j + 2)
                dve.tensor_tensor(du[:, j, :], dt[:, j, :], u[:, j, :], ALU.mult).then_inc(du_done, 1)
                for b in range(B):
                    dve.memset(decay[:, j, b * S:b * S + 1], 0.0).then_inc(yinit_done, 1)
                dve.tensor_scalar(y_acc[:, j, :], u[:, j, :], d_col[:, j:j + 1], None, ALU.mult).then_inc(yinit_done, 1)
            dve.wait_ge(wp_hi_done, 1)
            dve.scalar_tensor_tensor(out=wp_lo[:], in0=wp_f[:], scalar=W_SCALE, in1=wp_hi[:], op0=ALU.mult,
                                     op1=ALU.subtract).then_inc(wp_lo_done, 1)
            dve.wait_ge(late_loaded, 16 * 5)

            def qkv_low(i, unit):
                dve.wait_ge(qkv_hi, 4 * i + unit + 1)
                o, hi, n = ((q_lo[:, 0:512], q_hi[:, 0:512], 512), (q_lo[:, 512:1024], q_hi[:, 512:1024], 512),
                            (k_lo[:], k_hi[:], 256),
                            (v_lo[:].rearrange("p t d -> p (t d)"), v_hi[:].rearrange("p t d -> p (t d)"), 256))[unit]
                dve.scalar_tensor_tensor(out=o, in0=ps_qkv[:, 0:n], scalar=QKV_OUT, in1=hi, op0=ALU.mult,
                                         op1=ALU.subtract).then_inc(qkv_lo, 1)

            def row_max(i):
                dve.wait_ge(scores_ready, 3 * i + 1)
                dve.tensor_reduce(negmax[:, 0:QPG], ps_s0, AX.X, ALU.max, negate=True).then_inc(max_done, 1)
                dve.wait_ge(max_done, 3 * i + 1)
                dve.tensor_scalar(ebias[:, 0:QPG], negmax[:, 0:QPG], SCORE_SCALE, None, ALU.mult).then_inc(bias_ready, 1)
                for pair in range(2):
                    dve.wait_ge(scores_ready, 3 * i + 2 + pair)
                    dve.tensor_reduce(negmax[:, QPG + 2 * pair:QPG + 2 * pair + 2], ps_s1[pair], AX.X, ALU.max,
                                      negate=True).then_inc(max_done, 1)
                dve.wait_ge(max_done, 3 * i + 3)
                dve.tensor_scalar(ebias[:, QPG:], negmax[:, QPG:], SCORE_SCALE, None, ALU.mult).then_inc(bias_ready, 1)

            def recip(i, pair):
                dve.wait_ge(exp_done, 4 * i + 2 * pair + 2)
                dve.reciprocal(rsum[:, 2 * pair:2 * pair + 2, :], esum[:, 2 * pair:2 * pair + 2, :]).then_inc(rsum_ready, 1)

            def add_projection(i):
                dve.wait_ge(proj_done, 2 * i + 2)
                if not (isinstance(i, int) and i == 0):
                    dve.wait_ge(proj_added, i)
                r = resid[:, bass.ds(((i >> 2) & 3) * 2, 2), :].rearrange("p a n -> p (a n)")
                dve.scalar_tensor_tensor(out=r, in0=ps_proj[:], scalar=Y_OUT, in1=r, op0=ALU.mult,
                                         op1=ALU.add).then_inc(proj_added, 1)

            def pt_low(i, h):
                dve.wait_ge(pt_hi_done, 4 * i + h + 1)
                dve.tensor_tensor(pt_lo[:, h % 2, :], ps_pt[h % 2][:, 0:3 * P], pt_hi[:, h % 2, :],
                                  ALU.subtract).then_inc(pt_lo_done, 1)

            def o_low(i, pair):
                dve.wait_ge(o_hi_done, 2 * i + pair + 1)
                dve.scalar_tensor_tensor(out=o_lo[:, 2 * pair:2 * pair + 2, :].rearrange("p h s -> p (h s)"), in0=ps_o[:],
                                         scalar=O_OUT, in1=o_hi[:, 2 * pair:2 * pair + 2, :].rearrange("p h s -> p (h s)"),
                                         op0=ALU.mult, op1=ALU.subtract).then_inc(o_lo_done, 1)

            def scan(i, j):
                m = 2 * i + j
                dve.wait_ge(decay_ready, m + 1)
                dve.wait_ge(drive_ready, m + 1)
                if not (isinstance(i, int) and i == 0):
                    dve.wait_ge(acc_done, m - 1)
                dve.tensor_tensor_scan(h_st[:, j, 0:T], decay[:, j, :], drive[:, j, :], 0.0, ALU.mult,
                                       ALU.add).then_inc(scan_done, 1)

            def times_c(i, j):
                m = 2 * i + j
                dve.wait_ge(scan_done, m + 1)
                dve.wait_ge(c_loaded, 16 * i + 16)
                dve.tensor_tensor(h_st[:, j, 0:T], h_st[:, j, 0:T], c_row[:], ALU.mult).then_inc(hc_ready, 1)

            for unit in range(4):
                qkv_low(0, unit)

            def step(i, first=False, last=False):
                row_max(i)
                scan(i, 0)
                if not last:
                    qkv_low(i + 1, 0)
                recip(i, 0)
                times_c(i, 0)
                recip(i, 1)
                if not first:
                    add_projection(i - 1)
                if not last:
                    qkv_low(i + 1, 1)
                pt_low(i, 0)
                pt_low(i, 1)
                if not last:
                    qkv_low(i + 1, 2)
                scan(i, 1)
                o_low(i, 0)
                pt_low(i, 2)
                times_c(i, 1)
                pt_low(i, 3)
                o_low(i, 1)
                if not last:
                    qkv_low(i + 1, 3)

            step(0, first=True)
            with dve.Fori(1, NG - 1) as i:
                step(i)
            step(NG - 1, last=True)
            add_projection(NG - 1)
            dve.wait_ge(proj_added, NG)

            def moments(buf, nth, ready=None, per=1):
                for t in range(2 * B):
                    if ready is not None:
                        dve.wait_ge(ready, (t // per) + 1)
                    dve.bn_stats(stats[:, t, :], buf[:, t, :]).then_inc(st_done, 1)
                    if t % 2:
                        dve.wait_ge(st_done, 8 * nth + t + 1)
                        for s in (t - 1, t):
                            dve.bn_aggr(mv[:, s, :], stats[:, s, :]).then_inc(mv_done, 1)

            def normalise(buf, nth, done):
                for t in range(2 * B):
                    dve.wait_ge(rstd_done, 4 * nth + t // 2 + 1)
                    dve.tensor_scalar(buf[:, t, :], buf[:, t, :], mv[:, t, 0:1], rstd[:, t:t + 1], ALU.subtract,
                                      ALU.mult).then_inc(done, 1)

            moments(resid, 0)
            normalise(resid, 0, x1_ready)
            dve.wait_ge(acc_done, 2 * NS)
            for b in range(B):
                dve.wait_ge(z_ready, b + 1)
                dve.tensor_tensor(gated[:, 2 * b:2 * b + 2, :], y_acc[:, :, b * S:(b + 1) * S], z_silu[:, 2 * b:2 * b + 2, :],
                                  ALU.mult).then_inc(gated_ready, 1)
            dve.wait_ge(gated_ready, B)
            dve.wait_ge(x1_ready, 2 * B)
            for b in range(B):
                dve.wait_ge(gT_ready, b + 1)
                dve.tensor_tensor(res2[:, 2 * b:2 * b + 2, :], bank[b][:].rearrange("p (a n) -> p a n", a=2),
                                  resid[:, 2 * b:2 * b + 2, :], ALU.add).then_inc(res2_ready, 1)
            moments(res2, 1, res2_ready, 2)
            normalise(res2, 1, x2_ready)
            for b in range(B):
                n = 7 * b
                two = slice(2 * b, 2 * b + 2)
                dve.wait_ge(gates_done, B)
                for t in (2 * b, 2 * b + 1):
                    dve.max(top[:, t, :], bank[4][:, t * NE:(t + 1) * NE]).then_inc(route, 1)
                dve.wait_ge(route, n + 2)
                dve.tensor_tensor(top_d[:, two, :], top[:, two, 0:2], top[:, two, 0:1].broadcast_to((P, 2, 2)),
                                  ALU.subtract).then_inc(route, 1)
                dve.wait_ge(route_exp, b + 1)
                dve.tensor_tensor(top_s[:, two, :], top_e[:, two, 0:1], top_e[:, two, 1:2], ALU.add).then_inc(route, 1)
                dve.wait_ge(route, n + 4)
                dve.reciprocal(top_r[:, two, :], top_s[:, two, :]).then_inc(route, 1)
                dve.wait_ge(route, n + 5)
                dve.tensor_tensor(rw[:, two, :], top_e[:, two, :], top_r[:, two, :].broadcast_to((P, 2, 2)),
                                  ALU.mult).then_inc(route, 1)
                dve.wait_ge(route, n + 6)
                dve.tensor_tensor(rw_sum[:, two, :], rw[:, two, 0:1], rw[:, two, 1:2], ALU.add).then_inc(route, 1)
            dve.wait_ge(x2_ready, 2 * B)
            for t in range(2 * B):
                o = bank[(5, 6, 7, 0, 1, 2)[t % 6]]
                dve.wait_ge(moe_done, t + 1)
                dve.wait_ge(route, 7 * (t // 2) + 7)
                dve.scalar_tensor_tensor(out=res3[:, t, :], in0=o[:, HID:], scalar=rw_sum[:, t, :], in1=res2[:, t, :],
                                         op0=ALU.mult, op1=ALU.add).then_inc(mix_done, 1)
                dve.wait_ge(mix_done, 2 * t + 1)
                dve.tensor_tensor(res3[:, t, :], o[:, 0:HID], res3[:, t, :], ALU.add).then_inc(mix_done, 1)
            dve.wait_ge(mix_done, 4 * B)
            moments(res3, 2)
            normalise(res3, 2, y_ready)

        @block.gpsimd
        def _(pool):
            pool.memset(x_pad[:, :, :, 0:DC - 1], 0.0).then_inc(zeroed, 1)
            pool.memset(mask_f[:], 0.0).then_inc(consts, 1)
            pool.memset(mhalf[:], -0.5)
            pool.memset(ident[:], 0.0).then_inc(consts, 1)
            pool.wait_ge(consts, 2)
            pool.affine_select(out=ident[:], in_=ident[:], compare_op=ALU.not_equal, fill=1.0, base=0, pattern=[[-1, P]],
                               channel_multiplier=1).then_inc(zeroed, 1)
            pool.affine_select(out=mask_f[:], in_=mask_f[:], compare_op=ALU.is_ge, fill=MASKED, base=0, pattern=[[-1, P]],
                               channel_multiplier=1).then_inc(zeroed, 1)
            pool.wait_ge(zeroed, 3)
            pool.tensor_copy(ident_b[:], ident[:]).then_inc(consts, 1)
            pool.tensor_copy(mask_b[:], mask_f[:]).then_inc(consts, 1)
            pool.wait_ge(wq_loaded, 16)
            pool.wait_ge(wq_hi_done, 1)
            for g in range(1, NKV):
                w = slice(g * GW, (g + 1) * GW)
                pool.tensor_scalar(wqkv_hi[:, :, w], wqkv_f[:, :, w], W_SCALE, 1.0, ALU.mult, ALU.mult).then_inc(wq_hi_done, 1)
            pool.wait_ge(wp_loaded, 16)
            pool.tensor_scalar(wp_hi[:], wp_f[:], W_SCALE, 1.0, ALU.mult, ALU.mult).then_inc(wp_hi_done, 1)

            def drive_in(i, j):
                m = 2 * i + j
                pool.wait_ge(b_loaded, 16 * i + 16)
                if not (isinstance(i, int) and i == 0):
                    pool.wait_ge(scan_done, m - 1)
                pool.tensor_tensor(drive[:, j, :], du[:, j, :], b_row[:], ALU.mult).then_inc(drive_ready, 1)

            def accumulate(i, j):
                m = 2 * i + j
                pool.wait_ge(hc_ready, m + 1)
                if not (isinstance(i, int) and i == 0):
                    pool.wait_ge(acc_done, m - 1)
                pool.tensor_tensor(y_acc[:, j, :], y_acc[:, j, :], h_st[:, j, 0:T], ALU.add).then_inc(acc_done, 1)

            def probabilities(i, h):
                pool.wait_ge(rsum_ready, 2 * i + h // 2 + 1)
                pool.sem_inc(pool_turn, 1)
                pool.tensor_scalar(e_sb[:, h, 0:P], e_sb[:, h, 0:P], rsum[:, h, 0:1], P_SCALE, ALU.mult, ALU.mult)
                pool.tensor_scalar(e_sb[:, h, P:], e_sb[:, h, P:], rsum[:, h, 1:2], P_SCALE, ALU.mult,
                                   ALU.mult).then_inc(probs_ready, 1)

            pool.wait_ge(du_done, 3 * DT)
            pool.wait_ge(yinit_done, 2 + 8)
            drive_in(0, 0)
            drive_in(0, 1)

            def step(i, last=False):
                for h in range(QPG):
                    probabilities(i, h)
                for j in range(DT):
                    accumulate(i, j)
                    if not last:
                        drive_in(i + 1, j)

            step(0)
            with pool.Fori(1, NG - 1) as i:
                step(i)
            step(NG - 1, last=True)

            for nth in range(3):
                for b in range(B):
                    n = 4 * nth + b
                    two = slice(2 * b, 2 * b + 2)
                    pool.wait_ge(mv_done, 2 * n + 2)
                    pool.tensor_scalar(veps[:, two], mv[:, two, 1], EPS, None, ALU.add).then_inc(veps_done, 1)
                    pool.wait_ge(veps_done, n + 1)
                    pool.tensor_tensor(rstd[:, two], veps[:, two], mhalf[:, two], ALU.pow).then_inc(rstd_done, 1)


def kernel(x, ctx_1024, L0_attn_weight_qkv, L0_attn_weight_proj, L0_xattn_in_proj_w, L0_xattn_conv_w, L0_xattn_conv_b,
           L0_xattn_x_proj_w, L0_xattn_dt_proj_w, L0_xattn_dt_proj_b, L0_xattn_A_log, L0_xattn_D, L0_ffn_W_up, L0_ffn_W_down,
           L0_ffn_W_gate, L0_ffn_W_expert):
    import numpy as np
    import concourse.bacc as bacc
    from concourse.bass_utils import run_bass_kernel_spmd

    x2 = np.asarray(x).reshape(B * S, HID)
    layout = {
        "xT": x2.T, "x": x2, "wqkvT": np.asarray(L0_attn_weight_qkv).T, "wpT": np.asarray(L0_attn_weight_proj).T,
        "ctxT": np.asarray(ctx_1024).reshape(B * S, DM).T, "inT": np.asarray(L0_xattn_in_proj_w).T,
        "conv_w": np.asarray(L0_xattn_conv_w).reshape(2 * P, DC), "conv_b": L0_xattn_conv_b,
        "xprojT": np.asarray(L0_xattn_x_proj_w).T, "dtT": np.asarray(L0_xattn_dt_proj_w).T, "dt_b": L0_xattn_dt_proj_b,
        "A_log": L0_xattn_A_log, "D_skip": L0_xattn_D, "upT": np.asarray(L0_ffn_W_up).T, "downT": np.asarray(L0_ffn_W_down).T,
        "gateT": np.asarray(L0_ffn_W_gate).T, "expert": L0_ffn_W_expert,
    }
    nc = bacc.Bacc("TRN2", target_bir_lowering=False, num_devices=1)
    arrays, args = {}, []
    for name, a in layout.items():
        a = np.ascontiguousarray(a)
        arrays[f"in_{name}"] = a
        args.append(nc.dram_tensor(f"in_{name}", a.shape, mybir.dt.from_np(a.dtype), kind="ExternalInput").ap())
    args.append(nc.dram_tensor("out_y", (B, S, HID), F32, kind="ExternalOutput").ap())
    decoder_kernel(nc, *args)
    r = run_bass_kernel_spmd(nc, [arrays], core_ids=[0])
    return r.results[0]["out_y"]
```

```python
from contextlib import ExitStack

import concourse.bass as bass
from concourse import mybir

ALU = mybir.AluOpType
ACT = mybir.ActivationFunctionType
AX = mybir.AxisListType
F32 = mybir.dt.float32
F16 = mybir.dt.float16
BF16 = mybir.dt.bfloat16
I32 = mybir.dt.int32

P = 128
B, S, HID = 4, 256, 256
NH, NKV, D = 16, 4, 128
QPG = NH // NKV
GW = (QPG + 2) * D
NG = B * NKV
T = B * S
KT = HID // P
DM, NS, DC, DTR = 128, 16, 4, 8
DT = 256 // P
NE = 8
EPS = 1e-5
PE, ACTE, DVE, POOL = (mybir.EngineType.PE, mybir.EngineType.Activation, mybir.EngineType.DVE, mybir.EngineType.Pool)
LAG = 2

W_SCALE = 64.0
QK_OUT = float(D) ** -0.25 / W_SCALE
V_OUT = 1.0 / 16.0
Y_OUT = 1.0 / 256.0
MASKED = -3.0e38
SMALL = 0.01


def batch_group(i):
    return (i // NKV, i % NKV) if isinstance(i, int) else ((i >> 2) & 3, i & 3)


def decoder_kernel(nc, xT, x, wqkvT, wpT, ctxT, inT, conv_w, conv_b, xprojT, dtT, dt_b, A_log, D_skip,
                   upT, downT, gateT, expert, out):
    bc_rows = nc.dram_tensor("bc_rows", (2 * NS, T), F32, kind="Internal").ap()
    with ExitStack() as ctx:
        def sb(name, shape, dt=F32):
            return ctx.enter_context(nc.sbuf_tensor(name, shape, dt))

        def sem(name):
            return ctx.enter_context(nc.semaphore(name))

        xT_f = sb("xT_f", [P, KT, T])
        xT_hi = sb("xT_hi", [P, KT, T], F16)
        xT_lo = sb("xT_lo", [P, KT, T], F16)
        wqkv_f = sb("wqkv_f", [P, KT, NKV * GW])
        wqkv_hi = sb("wqkv_hi", [P, KT, NKV * GW], F16)
        wqkv_lo = sb("wqkv_lo", [P, KT, NKV * GW], F16)
        wp_f = sb("wp_f", [P, NH, HID])
        wp_hi = sb("wp_hi", [P, NH, HID], F16)
        wp_lo = sb("wp_lo", [P, NH, HID], F16)
        resid = sb("resid", [P, B * KT, HID])
        q_hi = sb("q_hi", [P, QPG * S], F16)
        q_lo = sb("q_lo", [P, QPG * S], F16)
        k_hi = sb("k_hi", [P, S], F16)
        k_lo = sb("k_lo", [P, S], F16)
        v_sb = sb("v_sb", [P, 2, D])
        e_sb = sb("e_sb", [P, QPG, 3 * P])
        pt_sb = sb("pt_sb", [P, 2, 3 * P])
        o_hi = sb("o_hi", [P, QPG, S], F16)
        o_lo = sb("o_lo", [P, QPG, S], F16)
        negmax = sb("negmax", [P, 2 * QPG])
        esum = sb("esum", [P, QPG, 2])
        rsum = sb("rsum", [P, QPG, 2])
        ident = sb("ident", [P, P])
        ident_b = sb("ident_b", [P, P], BF16)
        mask_f = sb("mask_f", [P, P])
        mask_b = sb("mask_b", [P, P], BF16)
        in_w = sb("in_w", [P, 2 * P])
        cw = sb("cw", [P, DT, DC])
        cb = sb("cb", [P, DT])
        xp_w = sb("xp_w", [P, DT, DTR + 2 * NS])
        dt_w = sb("dt_w", [DTR, 2 * P])
        dtb = sb("dtb", [P, DT])
        a_mat = sb("a_mat", [P, DT, NS])
        d_col = sb("d_col", [P, DT])
        u = sb("u", [P, DT, T])
        dt = sb("dt", [P, DT, T])
        du = sb("du", [P, DT, T])
        y_acc = sb("y_acc", [P, DT, T])
        decay = sb("decay", [P, DT, T])
        drive = sb("drive", [P, DT, T])
        h_st = sb("h_st", [P, DT, B * (S + DC - 1)])
        b_row = sb("b_row", [P, T])
        c_row = sb("c_row", [P, 2, T])
        xdbl = sb("xdbl", [DTR + 2 * NS, T])
        up_w = sb("up_w", [P, KT, HID])
        down_w = sb("down_w", [P, KT, HID])
        gate_w = sb("gate_w", [P, KT, NE])
        exp_w = sb("exp_w", [P, KT, HID])
        stats = sb("stats", [P, 2 * B, 6])
        mv = sb("mv", [P, 2 * B, 2])
        veps = sb("veps", [P, 2 * B])
        rstd = sb("rstd", [P, 2 * B])
        mhalf = sb("mhalf", [P, 2 * B])
        top = sb("top", [P, 2 * B, 8])
        top_d = sb("top_d", [P, 2 * B, 2])
        top_e = sb("top_e", [P, 2 * B, 2])
        top_s = sb("top_s", [P, 2 * B, 1])
        top_r = sb("top_r", [P, 2 * B, 1])
        rw = sb("rw", [P, 2 * B, 2])
        rw_sum = sb("rw_sum", [P, 2 * B, 1])

        ctx_sb = du[:, 0, :]
        x_pad = h_st[:].rearrange("p j (b l) -> p j b l", b=B)
        wq_flat = wqkv_f[:].rearrange("p k n -> p (k n)")
        z_silu = wq_flat[:, 0:2048].rearrange("p (t n) -> p t n", n=HID)
        gated = wq_flat[:, 2048:4096].rearrange("p (t n) -> p t n", n=HID)
        x2T = wq_flat[:, 4096:6144].rearrange("p (k t) -> p k t", k=KT)
        wp_flat = wp_f[:].rearrange("p h n -> p (h n)")
        hidden = wp_flat[:, 0:2048].rearrange("p (k t) -> p k t", k=KT)
        res3 = wp_flat[:, 2048:4096].rearrange("p (t n) -> p t n", n=HID)
        res2 = y_acc[:].rearrange("p j (t n) -> p (j t) n", n=HID)

        bank = [ctx.enter_context(nc.psum_tensor(f"bank{n}", [P, 512], F32)) for n in range(8)]
        ps_s0 = bank[0][:].rearrange("p (h t) -> p h t", h=QPG)
        ps_s1 = [bank[1 + n][:].rearrange("p (h t) -> p h t", h=2) for n in range(2)]
        ps_qkv, ps_proj, ps_o = bank[3], bank[4], bank[7]
        ps_pt = [bank[5], bank[6]]

        x_loaded, x_rest_loaded, wq0_loaded, wq_loaded, wp_loaded = (
            sem("x_loaded"), sem("x_rest_loaded"), sem("wq0_loaded"), sem("wq_loaded"), sem("wp_loaded"))
        ctx_loaded, cw_loaded, scanw_loaded, late_loaded = sem("ctx_loaded"), sem("cw_loaded"), sem("scanw_loaded"), sem("late_loaded")
        bc_stored, b_loaded, c_loaded, out_stored = sem("bc_stored"), sem("b_loaded"), sem("c_loaded"), sem("out_stored")
        pad_zeroed, consts, consts_b = sem("pad_zeroed"), sem("consts"), sem("consts_b")
        x_hi_done, x_lo_done, x_rest_lo = sem("x_hi_done"), sem("x_lo_done"), sem("x_rest_lo")
        wq_hi_done, wq_lo_done = sem("wq_hi_done"), sem("wq_lo_done")
        wp_hi_done, wp_lo_done = sem("wp_hi_done"), sem("wp_lo_done")
        in_done, pad_done, conv0_done, conv1_done, u_done = (sem("in_done"), sem("pad_done"), sem("conv0_done"),
                                                             sem("conv1_done"), sem("u_done"))
        xp_done, xdbl_done, dtp_done, dt_out = sem("xp_done"), sem("xdbl_done"), sem("dtp_done"), sem("dt_out")
        sp_exp, sp_ln, series, a_exp, a_done = sem("sp_exp"), sem("sp_ln"), sem("series"), sem("a_exp"), sem("a_done")
        dt_log, dt_ready, du_done = sem("dt_log"), sem("dt_ready"), sem("du_done")
        qk_ready, v_ready, qk_hi, qkv_out = sem("qk_ready"), sem("v_ready"), sem("qk_hi"), sem("qkv_out")
        scores_ready, max_done, exp_done = sem("scores_ready"), sem("max_done"), sem("exp_done")
        rsum_ready, probs_ready = sem("rsum_ready"), sem("probs_ready")
        pt_ready, pt_out = sem("pt_ready"), sem("pt_out")
        pv_done, o_hi_done, o_lo_done = sem("pv_done"), sem("o_hi_done"), sem("o_lo_done")
        proj_done, proj_added = sem("proj_done"), sem("proj_added")
        decay_ready, drive_ready, scan_done, hc_ready, acc_done = (sem("decay_ready"), sem("drive_ready"), sem("scan_done"),
                                                                   sem("hc_ready"), sem("acc_done"))
        st_done, mv_done, veps_done, rstd_done = sem("st_done"), sem("mv_done"), sem("veps_done"), sem("rstd_done")
        x1_ready, z_ready, gated_ready, gT_ready, res2_ready = (sem("x1_ready"), sem("z_ready"), sem("gated_ready"),
                                                                sem("gT_ready"), sem("res2_ready"))
        x2_ready, x2T_ps, x2T_ready = sem("x2_ready"), sem("x2T_ps"), sem("x2T_ready")
        up_done, relu_done, gates_done, moe_done = sem("up_done"), sem("relu_done"), sem("gates_done"), sem("moe_done")
        route, route_exp, mix_done, res3_ready, y_ready = (sem("route"), sem("route_exp"), sem("mix_done"),
                                                           sem("res3_ready"), sem("y_ready"))

        block = ctx.enter_context(nc.Block())

        def loop(engine, start, end):
            return nc.Fori(start, end, engines=[engine], hint_back_edge=True)

        @block.sync
        def _(sp):
            xT_v = xT.rearrange("(k p) t -> p k t", p=P)
            wq_v = wqkvT.rearrange("(k p) n -> p k n", p=P)
            sp.dma_start(xT_f[:, :, 0:S], xT_v[:, :, 0:S]).then_inc(x_loaded, 16)
            sp.dma_start(wqkv_f[:, :, 0:GW], wq_v[:, :, 0:GW]).then_inc(wq0_loaded, 16)
            sp.dma_start(ctx_sb, ctxT).then_inc(ctx_loaded, 16)
            sp.dma_start(in_w[:], inT).then_inc(ctx_loaded, 16)
            sp.dma_start(cw[:], conv_w.rearrange("(j p) k -> p j k", p=P)).then_inc(cw_loaded, 16)
            sp.dma_start(wqkv_f[:, :, GW:], wq_v[:, :, GW:]).then_inc(wq_loaded, 16)
            sp.dma_start(xp_w[:], xprojT.rearrange("(j p) n -> p j n", p=P)).then_inc(scanw_loaded, 16)
            sp.dma_start(dt_w[:], dtT).then_inc(scanw_loaded, 16)
            sp.dma_start(a_mat[:], A_log.rearrange("(j p) n -> p j n", p=P)).then_inc(scanw_loaded, 16)
            with nc.allow_non_contiguous_dma(reason="three short columns"):
                sp.dma_start(cb[:], conv_b.rearrange("(j p) -> p j", p=P)).then_inc(scanw_loaded, 16)
                sp.dma_start(dtb[:], dt_b.rearrange("(j p) -> p j", p=P)).then_inc(scanw_loaded, 16)
                sp.dma_start(d_col[:], D_skip.rearrange("(j p) -> p j", p=P)).then_inc(scanw_loaded, 16)
            sp.dma_start(wp_f[:], wpT.rearrange("(h p) n -> p h n", p=P)).then_inc(wp_loaded, 16)
            sp.dma_start(xT_f[:, :, S:], xT_v[:, :, S:]).then_inc(x_rest_loaded, 16)
            sp.dma_start(resid[:], x.rearrange("(t p) n -> p t n", p=P)).then_inc(late_loaded, 16)
            sp.dma_start(up_w[:], upT.rearrange("(k p) n -> p k n", p=P)).then_inc(late_loaded, 16)
            sp.dma_start(down_w[:], downT.rearrange("(k p) n -> p k n", p=P)).then_inc(late_loaded, 16)
            sp.dma_start(gate_w[:], gateT.rearrange("(k p) n -> p k n", p=P)).then_inc(late_loaded, 16)
            sp.dma_start(exp_w[:], expert.rearrange("(k p) n -> p k n", p=P)).then_inc(late_loaded, 16)
            sp.wait_ge(xdbl_done, 2)
            sp.dma_start(bc_rows, xdbl[DTR:, :]).then_inc(bc_stored, 16)
            sp.wait_ge(bc_stored, 16)
            sp.dma_start(b_row[:], bc_rows[0:1, :].broadcast_to((P, T))).then_inc(b_loaded, 16)
            sp.dma_start(c_row[:, 0, :], bc_rows[NS:NS + 1, :].broadcast_to((P, T))).then_inc(c_loaded, 16)
            sp.wait_ge(c_loaded, 16)
            sp.dma_start(c_row[:, 1, :], bc_rows[NS + 1:NS + 2, :].broadcast_to((P, T))).then_inc(c_loaded, 16)
            with sp.Fori(1, NS - 2, 2) as n:
                for m in range(2):
                    sp.wait_ge(drive_ready, 2 * n + 2 * m)
                    sp.dma_start(b_row[:], bc_rows[bass.ds(n + m, 1), :].broadcast_to((P, T))).then_inc(b_loaded, 16)
                    sp.wait_ge(c_loaded, 16 * n + 16 * (m + 1))
                    sp.wait_ge(hc_ready, 2 * n + 2 * m)
                    sp.dma_start(c_row[:, m, :], bc_rows[bass.ds(n + (NS + 1 + m), 1), :].broadcast_to((P, T))
                                 ).then_inc(c_loaded, 16)
            sp.wait_ge(drive_ready, 2 * NS - 2)
            sp.dma_start(b_row[:], bc_rows[NS - 1:NS, :].broadcast_to((P, T))).then_inc(b_loaded, 16)
            out_v = out.rearrange("b (a p) n -> b p a n", p=P)
            for b in range(B):
                sp.wait_ge(y_ready, 2 * b + 2)
                sp.dma_start(out_v[b], res3[:, 2 * b:2 * b + 2, :]).then_inc(out_stored, 16)
            sp.wait_ge(out_stored, 16 * B)

        @block.tensor
        def _(pe):
            def products(o, lhs, rhs, start=True, stop=True, skip=False):
                n = len(lhs)
                for k in range(n):
                    (lh, ll), (rh, rl) = lhs[k], rhs[k]
                    pe.matmul(o, lh, rh, start=start and k == 0, stop=False, skip_group_check=skip)
                    pe.matmul(o, lh, rl, start=False, stop=False, skip_group_check=skip)
                    m = pe.matmul(o, ll, rh, start=False, stop=stop and k == n - 1, skip_group_check=skip)
                return m

            def wq(g, off):
                return [(wqkv_hi[:, k, bass.ds(g * GW + off, D)], wqkv_lo[:, k, bass.ds(g * GW + off, D)]) for k in range(KT)]

            def xt(at, n):
                return [(xT_hi[:, k, bass.ds(at, n)], xT_lo[:, k, bass.ds(at, n)]) for k in range(KT)]

            def q_unit(i, pair):
                b, g = batch_group(i)
                for n in range(2):
                    m = products(ps_qkv[:, n * S:(n + 1) * S], wq(g, (2 * pair + n) * D), xt(b * S, S))
                m.then_inc(qk_ready, 1)

            def k_unit(i):
                b, g = batch_group(i)
                products(ps_qkv[:, 0:S], wq(g, QPG * D), xt(b * S, S)).then_inc(qk_ready, 1)

            def v_unit(i):
                b, g = batch_group(i)
                for t in range(2):
                    m = products(ps_qkv[:, t * D:(t + 1) * D], xt(b * S + t * P, P), wq(g, (QPG + 1) * D))
                m.then_inc(v_ready, 1)

            def scores(i):
                pe.matmul(ps_s0, ident_b[:], mask_b[:].unsqueeze(1).broadcast_to((P, QPG, P)),
                          start=True, stop=False, skip_group_check=True)
                for h in range(QPG):
                    m = products(ps_s0[:, h, :], [(q_hi[:, h * S:h * S + P], q_lo[:, h * S:h * S + P])],
                                 [(k_hi[:, 0:P], k_lo[:, 0:P])], start=False, skip=True)
                m.then_inc(scores_ready, 1)
                for pair in range(2):
                    o = ps_s1[pair]
                    pe.matmul(o[:, :, P:S], ident_b[:], mask_b[:].unsqueeze(1).broadcast_to((P, 2, P)),
                              start=True, stop=False, skip_group_check=True)
                    for n in range(2):
                        q0 = (2 * pair + n) * S + P
                        m = products(o[:, n, :], [(q_hi[:, q0:q0 + P], q_lo[:, q0:q0 + P])], [(k_hi[:], k_lo[:])],
                                     start=False, skip=True)
                    m.then_inc(scores_ready, 1)

            def transposes(i, h):
                k = 4 * i + h
                pe.wait_ge(probs_ready, k + 1)
                if not (isinstance(k, int) and k < 2):
                    pe.wait_ge(pt_out, k - 1)
                o = ps_pt[h % 2]
                pe.transpose(o[:, 0:P], e_sb[:, h, 0:P], ident[:])
                pe.transpose(o[:, P:2 * P], e_sb[:, h, P:2 * P], ident[:])
                pe.transpose(o[:, 2 * P:3 * P], e_sb[:, h, 2 * P:3 * P], ident[:]).then_inc(pt_ready, 1)

            def pv(i, h):
                k = 4 * i + h
                pe.wait_ge(pt_out, k + 1)
                if h % 2 == 0 and not (isinstance(k, int) and k == 0):
                    pe.wait_ge(o_lo_done, 2 * i + h // 2)
                o = ps_o[:, (h % 2) * S:(h % 2 + 1) * S]
                p_t = pt_sb[:, h % 2, :]
                pe.matmul(o, v_sb[:, 0, :], p_t[:, 0:S], start=True, stop=False, skip_group_check=True)
                pe.matmul(o[:, P:S], v_sb[:, 1, :], p_t[:, S:S + P], start=False, stop=True,
                          skip_group_check=True).then_inc(pv_done, 1)

            def project(i, pair):
                g = batch_group(i)[1]
                pe.wait_ge(o_lo_done, 2 * i + pair + 1)
                if pair == 0 and not (isinstance(i, int) and i == 0):
                    pe.wait_ge(proj_added, i)
                for n in range(2):
                    h = 2 * pair + n
                    w = [t[:, bass.ds(g * QPG + h, 1), :].rearrange("p a n -> p (a n)") for t in (wp_hi, wp_lo)]
                    for a in range(2):
                        m = products(ps_proj[:, a * HID:(a + 1) * HID],
                                     [(o_hi[:, h, a * P:(a + 1) * P], o_lo[:, h, a * P:(a + 1) * P])], [w],
                                     start=(h == 0 and a == 0), stop=(h == QPG - 1), skip=True)
                m.then_inc(proj_done, 1)

            def x_proj(c):
                for j in range(DT):
                    m = pe.matmul(ps_qkv[0:DTR + 2 * NS, :], xp_w[:, j, :], u[:, j, c * 512:(c + 1) * 512],
                                  start=j == 0, stop=j == DT - 1)
                m.then_inc(xp_done, 1)

            def dt_proj(j, c):
                pe.matmul(ps_qkv[:], dt_w[:, j * P:(j + 1) * P], xdbl[0:DTR, c * 512:(c + 1) * 512],
                          start=True, stop=True).then_inc(dtp_done, 1)

            pe.wait_ge(ctx_loaded, 32)
            for j in range(DT):
                for c in range(2):
                    pe.matmul(bank[4 + 2 * j + c][:], in_w[:, j * P:(j + 1) * P], ctx_sb[:, c * 512:(c + 1) * 512],
                              start=True, stop=True).then_inc(in_done, 1)
            pe.wait_ge(x_lo_done, 1)
            pe.wait_ge(wq_lo_done, 1)
            q_unit(0, 0)
            pe.wait_ge(qkv_out, 1)
            q_unit(0, 1)
            pe.wait_ge(qkv_out, 2)
            k_unit(0)
            pe.wait_ge(qkv_out, 3)
            v_unit(0)
            pe.wait_ge(consts_b, 2)
            scores(0)
            pe.wait_ge(pad_done, 4)

            def step(i, last=False, at=lambda place: None):
                transposes(i, 0)
                transposes(i, 1)
                pe.wait_ge(qkv_out, 4 * i + 4)
                at("q01")
                if not last:
                    q_unit(i + 1, 0)
                pv(i, 0)
                pv(i, 1)
                at("pv1")
                transposes(i, 2)
                transposes(i, 3)
                if not last:
                    pe.wait_ge(qkv_out, 4 * i + 5)
                    at("q23")
                    q_unit(i + 1, 1)
                at("pr01")
                project(i, 0)
                at("k")
                if not last:
                    pe.wait_ge(qkv_out, 4 * i + 6)
                    k_unit(i + 1)
                pv(i, 2)
                pv(i, 3)
                at("pv3")
                if not last:
                    pe.wait_ge(qkv_out, 4 * i + 7)
                    pe.wait_ge(exp_done, 4 * i + 4)
                    scores(i + 1)
                    at("v")
                    v_unit(i + 1)
                at("pr23")
                project(i, 1)
                at("end")

            def in_step0(place):
                if place == "q01":
                    pe.wait_ge(wq_lo_done, 2)
                elif place == "pr01":
                    pe.wait_ge(wp_lo_done, 1)
                elif place == "pr23":
                    pe.wait_ge(qkv_out, 8)
                    pe.wait_ge(scanw_loaded, 16 * 6)
                    pe.wait_ge(u_done, 2)
                    x_proj(0)
                elif place == "end":
                    pe.wait_ge(xdbl_done, 1)
                    x_proj(1)

            def in_step1(place):
                if place == "q01":
                    pe.wait_ge(wq_lo_done, 3)
                    pe.wait_ge(xdbl_done, 2)
                elif place == "pr01":
                    pe.wait_ge(wp_lo_done, 2)
                elif place == "pv1":
                    pe.wait_ge(qkv_out, 9)
                    dt_proj(0, 0)
                elif place == "q23":
                    pe.wait_ge(dt_out, 1)
                elif place == "k":
                    pe.wait_ge(qkv_out, 10)
                    dt_proj(0, 1)
                    pe.wait_ge(dt_out, 2)
                elif place == "pv3":
                    pe.wait_ge(qkv_out, 11)
                    dt_proj(1, 0)
                elif place == "v":
                    pe.wait_ge(dt_out, 3)
                elif place == "pr23":
                    pe.wait_ge(qkv_out, 12)
                    dt_proj(1, 1)
                elif place == "end":
                    pe.wait_ge(dt_out, 4)
                    pe.wait_ge(wq_lo_done, NKV)
                    pe.wait_ge(wp_lo_done, NKV)
                    pe.wait_ge(x_rest_lo, 2)

            step(0, at=in_step0)
            step(1, at=in_step1)
            with loop(PE, 2, NG - 1) as i:
                step(i)
            step(NG - 1, last=True)

            pe.wait_ge(late_loaded, 16 * 5)
            for b in range(B):
                pe.wait_ge(gated_ready, b + 1)
                for a in range(2):
                    for j in range(2):
                        m = pe.transpose(bank[b][:, a * HID + j * P:a * HID + (j + 1) * P],
                                         gated[:, 2 * b + j, a * P:(a + 1) * P], ident[:])
                m.then_inc(gT_ready, 1)
            pe.wait_ge(proj_added, NG)
            for b in range(B):
                pe.wait_ge(x2_ready, 2 * b + 2)
                for k in range(KT):
                    for a in range(2):
                        m = pe.transpose(bank[4 + b][:, k * S + a * P:k * S + (a + 1) * P],
                                         res2[:, 2 * b + a, k * P:(k + 1) * P], ident[:])
                m.then_inc(x2T_ps, 1)
            for b in range(B):
                pe.wait_ge(x2T_ready, b + 1)
                for o in range(2):
                    for k in range(KT):
                        m = pe.matmul(bank[b][:, o * S:(o + 1) * S], up_w[:, k, o * P:(o + 1) * P],
                                      x2T[:, k, b * S:(b + 1) * S], start=k == 0, stop=k == KT - 1)
                m.then_inc(up_done, 1)
                for t in range(2 * b, 2 * b + 2):
                    for k in range(KT):
                        m = pe.matmul(bank[4][:, t * NE:(t + 1) * NE], x2T[:, k, t * P:(t + 1) * P], gate_w[:, k, :],
                                      start=k == 0, stop=k == KT - 1)
                m.then_inc(gates_done, 1)
            for t in range(2 * B):
                o = bank[(5, 6, 7, 0, 1, 2)[t % 6]]
                pe.wait_ge(relu_done, t // 2 + 1 if t < 6 else B)
                if t == 3:
                    pe.wait_ge(relu_done, 3)
                if t >= 6:
                    pe.wait_ge(mix_done, 2 * (t - 5))
                for k in range(KT):
                    pe.matmul(o[:, 0:HID], hidden[:, k, t * P:(t + 1) * P], down_w[:, k, :], start=k == 0, stop=k == KT - 1)
                for k in range(KT):
                    m = pe.matmul(o[:, HID:], x2T[:, k, t * P:(t + 1) * P], exp_w[:, k, :], start=k == 0, stop=k == KT - 1)
                m.then_inc(moe_done, 1)

        @block.scalar
        def _(act):
            act.wait_ge(x_loaded, 16)
            act.activation(xT_hi[:, :, 0:S], xT_f[:, :, 0:S], ACT.Copy).then_inc(x_hi_done, 1)
            act.wait_ge(wq0_loaded, 16)
            act.activation(wqkv_hi[:, :, 0:GW], wqkv_f[:, :, 0:GW], ACT.Copy, scale=W_SCALE).then_inc(wq_hi_done, 1)
            for c in range(2):
                for j in range(DT):
                    act.wait_ge(in_done, 2 * j + c + 1)
                    act.activation(x_pad[:, j, 2 * c:2 * c + 2, DC - 1:],
                                   bank[4 + 2 * j + c][:].rearrange("p (b l) -> p b l", b=2), ACT.Copy).then_inc(pad_done, 1)

            def qk_high(i, unit):
                act.wait_ge(qk_ready, 3 * i + unit + 1)
                o, n = ((q_hi[:, 0:512], 512), (q_hi[:, 512:1024], 512), (k_hi[:], 256))[unit]
                act.activation(o, ps_qkv[:, 0:n], ACT.Copy, scale=QK_OUT).then_inc(qk_hi, 1)

            def exps(i, h):
                act.wait_ge(max_done, 3 * i + 1)
                if not (isinstance(i, int) and i == 0):
                    act.wait_ge(pt_ready, 4 * i + h - 3)
                act.activation(e_sb[:, h, 0:P], ps_s0[:, h, :], ACT.Exp, bias=negmax[:, h:h + 1], accum_out=esum[:, h, 0:1])
                act.wait_ge(max_done, 3 * i + 2 + h // 2)
                act.activation(e_sb[:, h, P:], ps_s1[h // 2][:, h % 2, :], ACT.Exp, bias=negmax[:, QPG + h:QPG + h + 1],
                               accum_out=esum[:, h, 1:2]).then_inc(exp_done, 1)

            def pt_copy(i, h):
                k = 4 * i + h
                act.wait_ge(pt_ready, k + 1)
                if not (isinstance(k, int) and k < 2):
                    act.wait_ge(pv_done, k - 1)
                act.activation(pt_sb[:, h % 2, :], ps_pt[h % 2][:, 0:3 * P], ACT.Copy).then_inc(pt_out, 1)

            def o_high(i, pair):
                act.wait_ge(pv_done, 4 * i + 2 * pair + 2)
                if not (isinstance(i, int) and i == 0):
                    act.wait_ge(proj_done, 2 * i + pair - 1)
                act.activation(o_hi[:, 2 * pair:2 * pair + 2, :].rearrange("p h s -> p (h s)"), ps_o[:],
                               ACT.Copy).then_inc(o_hi_done, 1)

            def scan_decay(n, j):
                act.wait_ge(scan_done, 2 * n + j + 1)
                act.activation(decay[:, j, :].rearrange("p (b l) -> p b l", b=B)[:, :, 1:],
                               dt[:, j, :].rearrange("p (b l) -> p b l", b=B)[:, :, 1:], ACT.Exp,
                               scale=a_mat[:, j, bass.ds(n, 1)]).then_inc(decay_ready, 1)

            for unit in range(3):
                qk_high(0, unit)
            act.wait_ge(x_rest_loaded, 16)
            act.activation(xT_hi[:, :, S:], xT_f[:, :, S:], ACT.Copy).then_inc(x_hi_done, 1)
            for h in range(QPG):
                exps(0, h)

            def step(i, slot, last=False):
                pt_copy(i, 0)
                pt_copy(i, 1)
                if not last:
                    qk_high(i + 1, 0)
                o_high(i, 0)
                pt_copy(i, 2)
                pt_copy(i, 3)
                if not last:
                    slot("q23")
                    qk_high(i + 1, 1)
                slot("k")
                if not last:
                    qk_high(i + 1, 2)
                slot("o")
                o_high(i, 1)
                if not last:
                    for h in range(QPG):
                        exps(i + 1, h)
                slot("end")

            def in_step0(slot):
                if slot == "k":
                    act.wait_ge(scanw_loaded, 16 * 6)
                    act.activation(a_mat[:], a_mat[:], ACT.Exp).then_inc(a_exp, 1)
                if slot == "o":
                    act.wait_ge(conv0_done, DC)
                    act.activation(u[:, 0, :], decay[:, 0, :], ACT.Silu, bias=cb[:, 0:1]).then_inc(u_done, 1)
                    act.wait_ge(conv1_done, 2 * DC - 1)
                    act.activation(u[:, 1, :], decay[:, 1, :], ACT.Silu, bias=cb[:, 1:2]).then_inc(u_done, 1)
                if slot == "end":
                    for c in range(2):
                        act.wait_ge(xp_done, c + 1)
                        act.activation(xdbl[:, c * 512:(c + 1) * 512], ps_qkv[0:DTR + 2 * NS, :],
                                       ACT.Copy).then_inc(xdbl_done, 1)

            def dt_copy(j, c):
                act.wait_ge(dtp_done, 2 * j + c + 1)
                w = slice(c * 512, (c + 1) * 512)
                act.activation(decay[:, j, w], ps_qkv[:], ACT.Abs, bias=dtb[:, j:j + 1])
                act.activation(du[:, j, w], ps_qkv[:], ACT.Relu, bias=dtb[:, j:j + 1]).then_inc(dt_out, 1)

            def soft_log(j):
                act.wait_ge(dt_out, 2 * j + 2)
                act.activation(decay[:, j, :], decay[:, j, :], ACT.Exp, scale=-1.0).then_inc(sp_exp, 1)
                act.wait_ge(sp_exp, j + 1)
                act.activation(dt[:, j, :], decay[:, j, :], ACT.Ln, bias=1.0).then_inc(sp_ln, 1)

            def in_step1(slot):
                if slot == "q23":
                    dt_copy(0, 0)
                if slot == "k":
                    dt_copy(0, 1)
                if slot == "o":
                    soft_log(0)
                    dt_copy(1, 0)
                if slot == "end":
                    dt_copy(1, 1)
                    soft_log(1)

            step(0, in_step0)
            step(1, in_step1)
            act.preload_act_table(ACT.Exp)
            act.wait_ge(a_done, 1)
            act.wait_ge(dt_ready, 2)

            def scan_slots(n):
                return lambda slot: scan_decay(n, "ko".index(slot)) if slot in "ko" else None

            with loop(ACTE, 2, NG - 1) as i:
                step(i, scan_slots(i - LAG))
            step(NG - 1, scan_slots(NG - 1 - LAG), last=True)
            for n in range(NS - LAG, NS):
                for j in range(DT):
                    scan_decay(n, j)

            for b in range(B):
                act.wait_ge(x1_ready, 2 * b + 2)
                act.activation(z_silu[:, 2 * b:2 * b + 2, :], resid[:, 2 * b:2 * b + 2, :], ACT.Silu).then_inc(z_ready, 1)
            for b in range(B):
                act.wait_ge(x2T_ps, b + 1)
                act.activation(x2T[:, :, b * S:(b + 1) * S], bank[4 + b][:].rearrange("p (k s) -> p k s", k=KT),
                               ACT.Copy).then_inc(x2T_ready, 1)
            for b in range(B):
                act.wait_ge(up_done, b + 1)
                act.activation(hidden[:, :, b * S:(b + 1) * S], bank[b][:].rearrange("p (k s) -> p k s", k=KT),
                               ACT.Relu).then_inc(relu_done, 1)
            for b in range(B):
                act.wait_ge(route, 7 * b + 3)
                act.activation(top_e[:, 2 * b:2 * b + 2, :], top_d[:, 2 * b:2 * b + 2, :], ACT.Exp).then_inc(route_exp, 1)

        @block.vector
        def _(dve):
            dve.wait_ge(x_hi_done, 1)
            dve.tensor_tensor(xT_lo[:, :, 0:S], xT_f[:, :, 0:S], xT_hi[:, :, 0:S], ALU.subtract).then_inc(x_lo_done, 1)

            def wq_low(g):
                dve.wait_ge(wq_hi_done, g + 1)
                w = slice(g * GW, (g + 1) * GW)
                dve.scalar_tensor_tensor(out=wqkv_lo[:, :, w], in0=wqkv_f[:, :, w], scalar=W_SCALE, in1=wqkv_hi[:, :, w],
                                         op0=ALU.mult, op1=ALU.subtract).then_inc(wq_lo_done, 1)

            def wp_low(g):
                dve.wait_ge(wp_hi_done, g + 1)
                w = slice(g * QPG, (g + 1) * QPG)
                dve.scalar_tensor_tensor(out=wp_lo[:, w, :], in0=wp_f[:, w, :], scalar=W_SCALE, in1=wp_hi[:, w, :],
                                         op0=ALU.mult, op1=ALU.subtract).then_inc(wp_lo_done, 1)

            def conv_tap(k):
                acc = decay[:, 0, :].rearrange("p (b l) -> p b l", b=B)
                if k == 0:
                    dve.wait_ge(cw_loaded, 16)
                    dve.wait_ge(pad_zeroed, 1)
                    dve.wait_ge(pad_done, 3)
                    dve.tensor_scalar(acc, x_pad[:, 0, :, 0:S], cw[:, 0, 0:1], None, ALU.mult).then_inc(conv0_done, 1)
                else:
                    dve.wait_ge(conv0_done, k)
                    dve.scalar_tensor_tensor(out=acc, in0=x_pad[:, 0, :, k:k + S], scalar=cw[:, 0, k:k + 1], in1=acc,
                                             op0=ALU.mult, op1=ALU.add).then_inc(conv0_done, 1)

            def qkv_low(i, unit):
                dve.wait_ge(qk_hi, 3 * i + unit + 1)
                o, hi, n = ((q_lo[:, 0:512], q_hi[:, 0:512], 512), (q_lo[:, 512:1024], q_hi[:, 512:1024], 512),
                            (k_lo[:], k_hi[:], 256))[unit]
                dve.scalar_tensor_tensor(out=o, in0=ps_qkv[:, 0:n], scalar=QK_OUT, in1=hi, op0=ALU.mult,
                                         op1=ALU.subtract).then_inc(qkv_out, 1)

            def v_copy(i):
                dve.wait_ge(v_ready, i + 1)
                dve.tensor_scalar(v_sb[:].rearrange("p t d -> p (t d)"), ps_qkv[:, 0:2 * D], V_OUT, None,
                                  ALU.mult).then_inc(qkv_out, 1)

            def row_max(i):
                for n, (o, ps) in enumerate(((negmax[:, 0:QPG], ps_s0), (negmax[:, QPG:QPG + 2], ps_s1[0]),
                                             (negmax[:, QPG + 2:], ps_s1[1]))):
                    dve.wait_ge(scores_ready, 3 * i + n + 1)
                    dve.tensor_reduce(o, ps, AX.X, ALU.max, negate=True).then_inc(max_done, 1)

            def normalise_probs(i, h):
                dve.wait_ge(exp_done, 4 * i + h + 1)
                dve.reciprocal(rsum[:, h, :], esum[:, h, :]).then_inc(rsum_ready, 1)
                dve.wait_ge(rsum_ready, 4 * i + h + 1)
                dve.tensor_scalar(e_sb[:, h, 0:P], e_sb[:, h, 0:P], rsum[:, h, 0:1], None, ALU.mult)
                dve.tensor_scalar(e_sb[:, h, P:], e_sb[:, h, P:], rsum[:, h, 1:2], None, ALU.mult).then_inc(probs_ready, 1)

            def add_projection(i):
                dve.wait_ge(proj_done, 2 * i + 2)
                if not (isinstance(i, int) and i == 0):
                    dve.wait_ge(proj_added, i)
                r = resid[:, bass.ds(batch_group(i)[0] * 2, 2), :].rearrange("p a n -> p (a n)")
                dve.scalar_tensor_tensor(out=r, in0=ps_proj[:], scalar=Y_OUT, in1=r, op0=ALU.mult,
                                         op1=ALU.add).then_inc(proj_added, 1)

            def o_low(i, pair):
                dve.wait_ge(o_hi_done, 2 * i + pair + 1)
                dve.tensor_tensor(o_lo[:, 2 * pair:2 * pair + 2, :].rearrange("p h s -> p (h s)"), ps_o[:],
                                  o_hi[:, 2 * pair:2 * pair + 2, :].rearrange("p h s -> p (h s)"),
                                  ALU.subtract).then_inc(o_lo_done, 1)

            def scan(n, j):
                m = 2 * n + j
                dve.wait_ge(decay_ready, m + 1)
                dve.wait_ge(drive_ready, m + 1)
                dve.wait_ge(acc_done, m + 1)
                dve.tensor_tensor_scan(h_st[:, j, 0:T], decay[:, j, :], drive[:, j, :], 0.0, ALU.mult,
                                       ALU.add).then_inc(scan_done, 1)

            def times_c(n, j):
                dve.wait_ge(scan_done, 2 * n + j + 3)
                dve.wait_ge(c_loaded, 16 * n + 16)
                dve.tensor_tensor(h_st[:, j, 0:T], h_st[:, j, 0:T], c_row[:, bass.ds(n & 1, 1), :].rearrange("p a t -> p (a t)"),
                                  ALU.mult).then_inc(hc_ready, 1)

            wq_low(0)
            conv_tap(0)
            conv_tap(1)
            qkv_low(0, 0)
            conv_tap(2)
            qkv_low(0, 1)
            conv_tap(3)
            qkv_low(0, 2)
            wq_low(1)
            row_max(0)
            normalise_probs(0, 0)
            v_copy(0)
            normalise_probs(0, 1)

            def step(i, slot, last=False):
                normalise_probs(i, 2)
                normalise_probs(i, 3)
                slot(0)
                if not last:
                    qkv_low(i + 1, 0)
                if not (isinstance(i, int) and i == 0):
                    add_projection(i - 1)
                o_low(i, 0)
                slot(1)
                if not last:
                    qkv_low(i + 1, 1)
                slot(2)
                if not last:
                    qkv_low(i + 1, 2)
                slot(3)
                o_low(i, 1)
                if not last:
                    row_max(i + 1)
                    normalise_probs(i + 1, 0)
                    v_copy(i + 1)
                    normalise_probs(i + 1, 1)

            def series_of(j):
                e, r, small = decay[:, j, :], drive[:, j, :], h_st[:, j, 0:T]
                dve.wait_ge(sp_exp, j + 1)
                dve.tensor_scalar(r, e, 1.0 / 3.0, None, ALU.mult).then_inc(series, 1)
                dve.wait_ge(series, 4 * j + 1)
                dve.scalar_tensor_tensor(out=r, in0=r, scalar=-0.5, in1=e, op0=ALU.add, op1=ALU.mult).then_inc(series, 1)
                dve.wait_ge(series, 4 * j + 2)
                dve.scalar_tensor_tensor(out=r, in0=r, scalar=1.0, in1=e, op0=ALU.add, op1=ALU.mult).then_inc(series, 1)
                dve.tensor_scalar(small, e, SMALL, None, ALU.is_lt).then_inc(series, 1)
                dve.wait_ge(series, 4 * j + 4)
                dve.wait_ge(sp_ln, j + 1)
                dve.copy_predicated(dt[:, j, :], small.bitcast(I32), r).then_inc(dt_log, 1)
                dve.wait_ge(dt_log, j + 1)
                dve.tensor_tensor(dt[:, j, :], dt[:, j, :], du[:, j, :], ALU.add).then_inc(dt_ready, 1)
                dve.memset(decay[:, j, :].rearrange("p (b l) -> p b l", b=B)[:, :, 0:1], 0.0).then_inc(scan_done, 1)

            def in_step0(slot):
                if slot == 0:
                    dve.wait_ge(late_loaded, 16 * 5)
                    wp_low(0)
                if slot == 1:
                    wq_low(2)
                    dve.wait_ge(a_exp, 1)
                    dve.tensor_scalar(a_mat[:], a_mat[:], -1.0, None, ALU.mult).then_inc(a_done, 1)
                if slot == 2:
                    wp_low(1)

            def in_step1(slot):
                if slot == 0:
                    wq_low(3)
                if slot == 1:
                    wp_low(2)
                if slot == 2:
                    wp_low(3)
                if slot == 3:
                    series_of(0)

            def scan_slots(n):
                def slot(s):
                    if s >= 2 or not (isinstance(n, int) and n == 0):
                        (scan, times_c)[s % 2](*((n - 1, 1) if s < 2 else (n, 0)))
                return slot

            step(0, in_step0)
            step(1, in_step1)
            series_of(1)
            step(LAG, scan_slots(0))
            with loop(DVE, LAG + 1, NG - 1) as i:
                step(i, scan_slots(i - LAG))
            step(NG - 1, scan_slots(NG - 1 - LAG), last=True)
            add_projection(NG - 1)
            dve.wait_ge(proj_added, NG)
            for n in range(NS - LAG, NS):
                for s in range(4):
                    scan_slots(n)(s)
            scan(NS - 1, 1)
            times_c(NS - 1, 1)

            def moments(buf, nth, ready=None, per=1):
                for t in range(2 * B):
                    if ready is not None:
                        dve.wait_ge(ready, (t // per) + 1)
                    dve.bn_stats(stats[:, t, :], buf[:, t, :]).then_inc(st_done, 1)
                    if t % 2:
                        dve.wait_ge(st_done, 8 * nth + t + 1)
                        for s in (t - 1, t):
                            dve.bn_aggr(mv[:, s, :], stats[:, s, :]).then_inc(mv_done, 1)

            def normalise(buf, nth, done):
                for t in range(2 * B):
                    dve.wait_ge(rstd_done, 4 * nth + t // 2 + 1)
                    dve.tensor_scalar(buf[:, t, :], buf[:, t, :], mv[:, t, 0:1], rstd[:, t:t + 1], ALU.subtract,
                                      ALU.mult).then_inc(done, 1)

            moments(resid, 0)
            normalise(resid, 0, x1_ready)
            dve.wait_ge(acc_done, 2 * NS + 2)
            for b in range(B):
                dve.wait_ge(z_ready, b + 1)
                dve.tensor_tensor(gated[:, 2 * b:2 * b + 2, :], y_acc[:, :, b * S:(b + 1) * S], z_silu[:, 2 * b:2 * b + 2, :],
                                  ALU.mult).then_inc(gated_ready, 1)
            dve.wait_ge(gated_ready, B)
            dve.wait_ge(x1_ready, 2 * B)
            for b in range(B):
                dve.wait_ge(gT_ready, b + 1)
                dve.tensor_tensor(res2[:, 2 * b:2 * b + 2, :], bank[b][:].rearrange("p (a n) -> p a n", a=2),
                                  resid[:, 2 * b:2 * b + 2, :], ALU.add).then_inc(res2_ready, 1)
            moments(res2, 1, res2_ready, 2)
            normalise(res2, 1, x2_ready)
            for b in range(B):
                n = 7 * b
                two = slice(2 * b, 2 * b + 2)
                dve.wait_ge(gates_done, B)
                for t in (2 * b, 2 * b + 1):
                    dve.max(top[:, t, :], bank[4][:, t * NE:(t + 1) * NE]).then_inc(route, 1)
                dve.wait_ge(route, n + 2)
                dve.tensor_tensor(top_d[:, two, :], top[:, two, 0:2], top[:, two, 0:1].broadcast_to((P, 2, 2)),
                                  ALU.subtract).then_inc(route, 1)
                dve.wait_ge(route_exp, b + 1)
                dve.tensor_tensor(top_s[:, two, :], top_e[:, two, 0:1], top_e[:, two, 1:2], ALU.add).then_inc(route, 1)
                dve.wait_ge(route, n + 4)
                dve.reciprocal(top_r[:, two, :], top_s[:, two, :]).then_inc(route, 1)
                dve.wait_ge(route, n + 5)
                dve.tensor_tensor(rw[:, two, :], top_e[:, two, :], top_r[:, two, :].broadcast_to((P, 2, 2)),
                                  ALU.mult).then_inc(route, 1)
                dve.wait_ge(route, n + 6)
                dve.tensor_tensor(rw_sum[:, two, :], rw[:, two, 0:1], rw[:, two, 1:2], ALU.add).then_inc(route, 1)
            dve.wait_ge(x2_ready, 2 * B)
            for t in range(2 * B):
                o = bank[(5, 6, 7, 0, 1, 2)[t % 6]]
                dve.wait_ge(moe_done, t + 1)
                dve.wait_ge(route, 7 * (t // 2) + 7)
                dve.scalar_tensor_tensor(out=res3[:, t, :], in0=o[:, HID:], scalar=rw_sum[:, t, :], in1=res2[:, t, :],
                                         op0=ALU.mult, op1=ALU.add).then_inc(mix_done, 1)
                dve.wait_ge(mix_done, 2 * t + 1)
                dve.tensor_tensor(res3[:, t, :], o[:, 0:HID], res3[:, t, :], ALU.add).then_inc(mix_done, 1)
            dve.wait_ge(mix_done, 4 * B)
            moments(res3, 2)
            normalise(res3, 2, y_ready)

        @block.gpsimd
        def _(pool):
            pool.memset(x_pad[:, :, :, 0:DC - 1], 0.0).then_inc(pad_zeroed, 1)
            pool.memset(mask_f[:], 0.0).then_inc(consts, 1)
            pool.memset(mhalf[:], -0.5)
            pool.memset(ident[:], 0.0).then_inc(consts, 1)
            pool.wait_ge(consts, 2)
            pool.affine_select(out=ident[:], in_=ident[:], compare_op=ALU.not_equal, fill=1.0, base=0, pattern=[[-1, P]],
                               channel_multiplier=1).then_inc(consts, 1)
            pool.affine_select(out=mask_f[:], in_=mask_f[:], compare_op=ALU.is_ge, fill=MASKED, base=0, pattern=[[-1, P]],
                               channel_multiplier=1).then_inc(consts, 1)
            pool.wait_ge(consts, 4)
            pool.tensor_copy(ident_b[:], ident[:]).then_inc(consts_b, 1)
            pool.tensor_copy(mask_b[:], mask_f[:]).then_inc(consts_b, 1)

            def wq_high(g):
                w = slice(g * GW, (g + 1) * GW)
                pool.tensor_scalar(wqkv_hi[:, :, w], wqkv_f[:, :, w], W_SCALE, 1.0, ALU.mult, ALU.mult).then_inc(wq_hi_done, 1)

            def wp_high(g):
                w = slice(g * QPG, (g + 1) * QPG)
                pool.tensor_scalar(wp_hi[:, w, :], wp_f[:, w, :], W_SCALE, 1.0, ALU.mult, ALU.mult).then_inc(wp_hi_done, 1)

            def conv_tap(k):
                acc = decay[:, 1, :].rearrange("p (b l) -> p b l", b=B)
                tap = drive[:, 1, :].rearrange("p (b l) -> p b l", b=B)
                if k == 0:
                    pool.wait_ge(pad_done, 4)
                else:
                    pool.wait_ge(conv1_done, 2 * k - 1)
                pool.tensor_scalar(acc if k == 0 else tap, x_pad[:, 1, :, k:k + S], cw[:, 1, k:k + 1], 1.0, ALU.mult,
                                   ALU.mult).then_inc(conv1_done, 1)
                if k:
                    pool.wait_ge(conv1_done, 2 * k)
                    pool.tensor_tensor(acc, acc, tap, ALU.add).then_inc(conv1_done, 1)

            pool.wait_ge(cw_loaded, 16)
            pool.wait_ge(wq_loaded, 16)
            pool.wait_ge(wq_hi_done, 1)
            wq_high(1)
            pool.wait_ge(wp_loaded, 16)
            wp_high(0)
            for k in range(DC):
                conv_tap(k)
            wq_high(2)
            wp_high(1)
            wq_high(3)
            wp_high(2)
            wp_high(3)
            pool.wait_ge(x_hi_done, 2)
            for k in range(KT):
                pool.tensor_tensor(xT_lo[:, k, S:], xT_f[:, k, S:], xT_hi[:, k, S:], ALU.subtract).then_inc(x_rest_lo, 1)
            pool.wait_ge(scanw_loaded, 16 * 6)
            for j in range(DT):
                pool.wait_ge(u_done, j + 1)
                pool.tensor_scalar(y_acc[:, j, :], u[:, j, :], d_col[:, j:j + 1], 1.0, ALU.mult, ALU.mult).then_inc(acc_done, 1)
            for j in range(DT):
                pool.wait_ge(dt_ready, j + 1)
                pool.tensor_tensor(du[:, j, :], dt[:, j, :], u[:, j, :], ALU.mult).then_inc(du_done, 1)

            def drive_in(n, j):
                pool.wait_ge(b_loaded, 16 * n + 16)
                pool.wait_ge(scan_done, 2 * n + j + 1)
                pool.tensor_tensor(drive[:, j, :], du[:, j, :], b_row[:], ALU.mult).then_inc(drive_ready, 1)

            def accumulate(n, j):
                pool.wait_ge(hc_ready, 2 * n + j + 1)
                pool.wait_ge(acc_done, 2 * n + j + 1)
                pool.tensor_tensor(y_acc[:, j, :], y_acc[:, j, :], h_st[:, j, 0:T], ALU.add).then_inc(acc_done, 1)

            pool.wait_ge(du_done, DT)
            for j in range(DT):
                drive_in(0, j)
            with loop(POOL, 0, NS - 1) as n:
                for j in range(DT):
                    accumulate(n, j)
                    drive_in(n + 1, j)
            for j in range(DT):
                accumulate(NS - 1, j)

            for nth in range(3):
                for b in range(B):
                    n = 4 * nth + b
                    two = slice(2 * b, 2 * b + 2)
                    pool.wait_ge(mv_done, 2 * n + 2)
                    pool.tensor_scalar(veps[:, two], mv[:, two, 1], EPS, None, ALU.add).then_inc(veps_done, 1)
                    pool.wait_ge(veps_done, n + 1)
                    pool.tensor_tensor(rstd[:, two], veps[:, two], mhalf[:, two], ALU.pow).then_inc(rstd_done, 1)


def kernel(x, ctx_1024, L0_attn_weight_qkv, L0_attn_weight_proj, L0_xattn_in_proj_w, L0_xattn_conv_w, L0_xattn_conv_b,
           L0_xattn_x_proj_w, L0_xattn_dt_proj_w, L0_xattn_dt_proj_b, L0_xattn_A_log, L0_xattn_D, L0_ffn_W_up, L0_ffn_W_down,
           L0_ffn_W_gate, L0_ffn_W_expert):
    import numpy as np
    import concourse.bacc as bacc
    from concourse.bass_utils import run_bass_kernel_spmd

    x2 = np.asarray(x).reshape(B * S, HID)
    layout = {
        "xT": x2.T, "x": x2, "wqkvT": np.asarray(L0_attn_weight_qkv).T, "wpT": np.asarray(L0_attn_weight_proj).T,
        "ctxT": np.asarray(ctx_1024).reshape(B * S, DM).T, "inT": np.asarray(L0_xattn_in_proj_w).T,
        "conv_w": np.asarray(L0_xattn_conv_w).reshape(2 * P, DC), "conv_b": L0_xattn_conv_b,
        "xprojT": np.asarray(L0_xattn_x_proj_w).T, "dtT": np.asarray(L0_xattn_dt_proj_w).T, "dt_b": L0_xattn_dt_proj_b,
        "A_log": L0_xattn_A_log, "D_skip": L0_xattn_D, "upT": np.asarray(L0_ffn_W_up).T, "downT": np.asarray(L0_ffn_W_down).T,
        "gateT": np.asarray(L0_ffn_W_gate).T, "expert": L0_ffn_W_expert,
    }
    nc = bacc.Bacc("TRN2", target_bir_lowering=False, num_devices=1)
    arrays, args = {}, []
    for name, a in layout.items():
        a = np.ascontiguousarray(a)
        arrays[f"in_{name}"] = a
        args.append(nc.dram_tensor(f"in_{name}", a.shape, mybir.dt.from_np(a.dtype), kind="ExternalInput").ap())
    args.append(nc.dram_tensor("out_y", (B, S, HID), F32, kind="ExternalOutput").ap())
    decoder_kernel(nc, *args)
    r = run_bass_kernel_spmd(nc, [arrays], core_ids=[0])
    return r.results[0]["out_y"]
```

```python
from contextlib import ExitStack

import concourse.bass as bass
from concourse import mybir

ALU = mybir.AluOpType
ACT = mybir.ActivationFunctionType
AX = mybir.AxisListType
F32 = mybir.dt.float32
F16 = mybir.dt.float16
BF16 = mybir.dt.bfloat16
I32 = mybir.dt.int32

P = 128
B, S, HID = 4, 256, 256
NH, NKV, D = 16, 4, 128
QPG = NH // NKV
GW = (QPG + 2) * D
NG = B * NKV
T = B * S
KT = HID // P
DM, NS, DC, DTR = 128, 16, 4, 8
DT = 256 // P
NE = 8
EPS = 1e-5
PE, ACTE, DVE, POOL = (mybir.EngineType.PE, mybir.EngineType.Activation, mybir.EngineType.DVE, mybir.EngineType.Pool)
LAG = 3
PE_TILE = DT * (NG - 1 - LAG) - 1
TILES = DT * NS

W_SCALE = 64.0
QK_OUT = float(D) ** -0.25 / W_SCALE
V_OUT = 1.0 / 16.0
Y_OUT = 1.0 / 256.0
MASKED = -3.0e38
SMALL = 0.01


def batch_of(i):
    return i // NKV if isinstance(i, int) else i >> 2


def decoder_kernel(nc, xT, x, wqkvT, wpT, ctxT, inT, conv_w, conv_b, xprojT, dtT, dt_b, A_log, D_skip,
                   upT, downT, gateT, expert, out):
    bc_rows = nc.dram_tensor("bc_rows", (2 * NS, T), F32, kind="Internal").ap()
    with ExitStack() as ctx:
        def sb(name, shape, dt=F32):
            return ctx.enter_context(nc.sbuf_tensor(name, shape, dt))

        def sem(name):
            return ctx.enter_context(nc.semaphore(name))

        xT_f = sb("xT_f", [P, KT, T])
        xT_hi = sb("xT_hi", [P, KT, T], F16)
        xT_lo = sb("xT_lo", [P, KT, T], F16)
        wqkv_f = sb("wqkv_f", [P, KT, NKV * GW])
        wqkv_hi = sb("wqkv_hi", [P, KT, NKV * GW], F16)
        wqkv_lo = sb("wqkv_lo", [P, KT, NKV * GW], F16)
        wp_f = sb("wp_f", [P, NH, HID])
        wp_hi = sb("wp_hi", [P, NH, HID], F16)
        wp_lo = sb("wp_lo", [P, NH, HID], F16)
        resid = sb("resid", [P, B * S // P, HID])
        q_hi = sb("q_hi", [P, QPG * S], F16)
        q_lo = sb("q_lo", [P, QPG * S], F16)
        k_hi = sb("k_hi", [P, S], F16)
        k_lo = sb("k_lo", [P, S], F16)
        v_sb = sb("v_sb", [P, 2, D])
        e_sb = sb("e_sb", [P, QPG, 3 * P])
        pt_sb = sb("pt_sb", [P, 2, 3 * P])
        o_hi = sb("o_hi", [P, QPG, S], F16)
        o_lo = sb("o_lo", [P, QPG, S], F16)
        negmax = sb("negmax", [P, 2 * QPG])
        esum = sb("esum", [P, QPG, 2])
        rsum = sb("rsum", [P, QPG, 2])
        ident = sb("ident", [P, P])
        ident_b = sb("ident_b", [P, P], BF16)
        mask_f = sb("mask_f", [P, P])
        mask_b = sb("mask_b", [P, P], BF16)
        in_w = sb("in_w", [P, 2 * P])
        cw = sb("cw", [P, DT, DC])
        cb = sb("cb", [P, DT])
        xp_w = sb("xp_w", [P, DT, DTR + 2 * NS])
        dt_w = sb("dt_w", [DTR, 2 * P])
        dtb = sb("dtb", [P, DT])
        a_mat = sb("a_mat", [P, DT, NS])
        d_col = sb("d_col", [P, DT])
        u = sb("u", [P, DT, T])
        dt = sb("dt", [P, DT, T])
        du = sb("du", [P, DT, T])
        y_acc = sb("y_acc", [P, DT, T])
        decay = sb("decay", [P, DT, T])
        drive = sb("drive", [P, DT, T])
        h_st = sb("h_st", [P, DT, B * (S + DC - 1)])
        b_row = sb("b_row", [P, 2, T])
        c_row = sb("c_row", [P, 2, T])
        xdbl = sb("xdbl", [DTR + 2 * NS, T])
        exp_w = sb("exp_w", [P, KT, HID + NE])
        stats = sb("stats", [P, 2 * B, 6])
        mv = sb("mv", [P, 2 * B, 2])
        rstd = sb("rstd", [P, 2 * B])
        veps = sb("veps", [P, 2 * B])
        mhalf = sb("mhalf", [P, 2 * B])
        shift = sb("shift", [P, 2 * B])
        top = sb("top", [P, 2 * B, 8])
        top_d = sb("top_d", [P, 2 * B, 2])
        top_e = sb("top_e", [P, 2 * B, 2])
        top_s = sb("top_s", [P, 2 * B, 1])
        top_r = sb("top_r", [P, 2 * B, 1])
        rw = sb("rw", [P, 2 * B, 2])
        rw_sum = sb("rw_sum", [P, 2 * B, 1])

        ctx_sb = du[:, 0, :]
        x_pad = h_st[:].rearrange("p j (b l) -> p j b l", b=B)
        up_w = xT_f[:, :, 0:HID]
        down_w = xT_f[:, :, HID:2 * HID]
        wq_flat = wqkv_f[:].rearrange("p k n -> p (k n)")
        z_silu = wq_flat[:, 0:2048].rearrange("p (t n) -> p t n", n=HID)
        gated = wq_flat[:, 2048:4096].rearrange("p (t n) -> p t n", n=HID)
        x2T = wq_flat[:, 4096:6144].rearrange("p (k t) -> p k t", k=KT)
        wp_flat = wp_f[:].rearrange("p h n -> p (h n)")
        hidden = wp_flat[:, 0:2048].rearrange("p (k t) -> p k t", k=KT)
        res3 = wp_flat[:, 2048:4096].rearrange("p (t n) -> p t n", n=HID)
        res2 = y_acc[:].rearrange("p j (t n) -> p (j t) n", n=HID)

        y_ps = ctx.enter_context(nc.psum_tensor("y_ps", [P, 4, 512], F32))
        bank = [y_ps[:, n, :] for n in range(4)]
        bank += [ctx.enter_context(nc.psum_tensor(f"bank{n}", [P, 512], F32))[:] for n in range(4, 8)]
        ps_s0 = bank[0][:].rearrange("p (h t) -> p h t", h=QPG)
        ps_s1 = [bank[1 + n][:].rearrange("p (h t) -> p h t", h=2) for n in range(2)]
        ps_proj, ps_o = bank[4], bank[7]
        ps_pt = [bank[5], bank[6]]

        x_loaded, x_rest_loaded = sem("x_loaded"), sem("x_rest_loaded")
        wq0_loaded, wq1_loaded, wq_loaded = sem("wq0_loaded"), sem("wq1_loaded"), sem("wq_loaded")
        wp0_loaded, wp_loaded = sem("wp0_loaded"), sem("wp_loaded")
        ctx_loaded, cw_loaded, scanw_loaded, late_loaded = sem("ctx_loaded"), sem("cw_loaded"), sem("scanw_loaded"), sem("late_loaded")
        ffn_loaded = sem("ffn_loaded")
        bc_stored, b_loaded, c_loaded, out_stored = sem("bc_stored"), sem("b_loaded"), sem("c_loaded"), sem("out_stored")
        pad_zeroed, consts, consts_b = sem("pad_zeroed"), sem("consts"), sem("consts_b")
        x_hi_done, x_lo_done, x_rest_lo = sem("x_hi_done"), sem("x_lo_done"), sem("x_rest_lo")
        wq_hi_done, wq_lo_done = sem("wq_hi_done"), sem("wq_lo_done")
        wp_hi_done, wp_lo_done = sem("wp_hi_done"), sem("wp_lo_done")
        in_done, pad_done, conv0_done, conv1_done, u_done = (sem("in_done"), sem("pad_done"), sem("conv0_done"),
                                                             sem("conv1_done"), sem("u_done"))
        xp_done, xdbl_done, dtp_done, dt_out = sem("xp_done"), sem("xdbl_done"), sem("dtp_done"), sem("dt_out")
        sp_exp, sp_ln, series0, a_exp, a_done = sem("sp_exp"), sem("sp_ln"), sem("series0"), sem("a_exp"), sem("a_done")
        zero_done = sem("zero_done")
        series1, dt_small, dt_log, dt_ready, du_done = sem("series1"), sem("dt_small"), sem("dt_log"), sem("dt_ready"), sem("du_done")
        qk_ready, v_ready, qk_hi, qk_out, v_out = (sem("qk_ready"), sem("v_ready"), sem("qk_hi"), sem("qk_out"),
                                                   sem("v_out"))
        scores_ready, max_done, exp_done = sem("scores_ready"), sem("max_done"), sem("exp_done")
        rsum_ready, probs_ready = sem("rsum_ready"), sem("probs_ready")
        pt_ready, pt_out = sem("pt_ready"), sem("pt_out")
        pv_done, o_hi_done, o_lo_done = sem("pv_done"), sem("o_hi_done"), sem("o_lo_done")
        proj_done, proj_added = sem("proj_done"), sem("proj_added")
        decay_ready, drive_ready, scan_done, hc_ready, hc_last, acc_done, ysum_done = (
            sem("decay_ready"), sem("drive_ready"), sem("scan_done"), sem("hc_ready"), sem("hc_last"), sem("acc_done"), sem("ysum_done"))
        st_done, mv_done, veps_done = sem("st_done"), sem("mv_done"), sem("veps_done")
        rstd_done, shift_done = sem("rstd_done"), sem("shift_done")
        x1_ready, z_ready, gated_ready, gT_ready, res2_ready = (sem("x1_ready"), sem("z_ready"), sem("gated_ready"),
                                                                sem("gT_ready"), sem("res2_ready"))
        x2_ready, x2T_ps, x2T_ready = sem("x2_ready"), sem("x2T_ps"), sem("x2T_ready")
        up_done, relu_done, expert_done, down_done = sem("up_done"), sem("relu_done"), sem("expert_done"), sem("down_done")
        route, route_exp = sem("route"), sem("route_exp")
        expert_mixed, shared_mixed = sem("expert_mixed"), sem("shared_mixed")
        y_ready, y_last_ready = sem("y_ready"), sem("y_last_ready")

        def ps_qkv(i, unit):
            return bank[3 + unit if isinstance(i, int) and i == 0 else 3]

        block = ctx.enter_context(nc.Block())

        def loop(engine, start, end, step=1):
            return nc.Fori(start, end, step, engines=[engine], hint_back_edge=True)

        @block.sync
        def _(sp):
            xT_v = xT.rearrange("(k p) t -> p k t", p=P)
            wq_v = wqkvT.rearrange("(k p) n -> p k n", p=P)
            wp_v = wpT.rearrange("(h p) n -> p h n", p=P)
            sp.dma_start(ctx_sb, ctxT).then_inc(ctx_loaded, 16)
            sp.dma_start(in_w[:], inT).then_inc(ctx_loaded, 16)
            sp.dma_start(xT_f[:, :, 0:S], xT_v[:, :, 0:S]).then_inc(x_loaded, 16)
            sp.dma_start(wqkv_f[:, :, 0:GW], wq_v[:, :, 0:GW]).then_inc(wq0_loaded, 16)
            sp.dma_start(cw[:], conv_w.rearrange("(j p) k -> p j k", p=P)).then_inc(cw_loaded, 16)
            sp.dma_start(wqkv_f[:, :, GW:2 * GW], wq_v[:, :, GW:2 * GW]).then_inc(wq1_loaded, 16)
            sp.dma_start(wp_f[:, 0:QPG, :], wp_v[:, 0:QPG, :]).then_inc(wp0_loaded, 16)
            with nc.allow_non_contiguous_dma(reason="three short columns"):
                sp.dma_start(cb[:], conv_b.rearrange("(j p) -> p j", p=P)).then_inc(scanw_loaded, 16)
                sp.dma_start(dtb[:], dt_b.rearrange("(j p) -> p j", p=P)).then_inc(scanw_loaded, 16)
                sp.dma_start(d_col[:], D_skip.rearrange("(j p) -> p j", p=P)).then_inc(scanw_loaded, 16)
            sp.dma_start(xp_w[:], xprojT.rearrange("(j p) n -> p j n", p=P)).then_inc(scanw_loaded, 16)
            sp.dma_start(dt_w[:], dtT).then_inc(scanw_loaded, 16)
            sp.dma_start(a_mat[:], A_log.rearrange("(j p) n -> p j n", p=P)).then_inc(scanw_loaded, 16)
            sp.dma_start(wqkv_f[:, :, 2 * GW:], wq_v[:, :, 2 * GW:]).then_inc(wq_loaded, 16)
            sp.dma_start(wp_f[:, QPG:, :], wp_v[:, QPG:, :]).then_inc(wp_loaded, 16)
            sp.dma_start(xT_f[:, :, S:], xT_v[:, :, S:]).then_inc(x_rest_loaded, 16)
            sp.dma_start(resid[:], x.rearrange("(t p) n -> p t n", p=P)).then_inc(late_loaded, 16)
            sp.dma_start(exp_w[:, :, HID:], gateT.rearrange("(k p) n -> p k n", p=P)).then_inc(late_loaded, 16)
            sp.dma_start(exp_w[:, :, 0:HID], expert.rearrange("(k p) n -> p k n", p=P)).then_inc(late_loaded, 16)
            sp.wait_ge(x_rest_lo, 2)
            sp.dma_start(up_w, upT.rearrange("(k p) n -> p k n", p=P)).then_inc(ffn_loaded, 16)
            sp.dma_start(down_w, downT.rearrange("(k p) n -> p k n", p=P)).then_inc(ffn_loaded, 16)
            sp.wait_ge(xdbl_done, 2)
            sp.dma_start(bc_rows, xdbl[DTR:, :]).then_inc(bc_stored, 16)
            sp.wait_ge(bc_stored, 16)
            sp.dma_start(b_row[:, 0, :], bc_rows[0:1, :].broadcast_to((P, T))).then_inc(b_loaded, 16)
            sp.dma_start(c_row[:, 0, :], bc_rows[NS:NS + 1, :].broadcast_to((P, T))).then_inc(c_loaded, 16)
            sp.wait_ge(b_loaded, 16)
            sp.dma_start(b_row[:, 1, :], bc_rows[1:2, :].broadcast_to((P, T))).then_inc(b_loaded, 16)
            sp.wait_ge(c_loaded, 16)
            sp.dma_start(c_row[:, 1, :], bc_rows[NS + 1:NS + 2, :].broadcast_to((P, T))).then_inc(c_loaded, 16)
            looped = NS - 4
            with sp.Fori(1, looped - 1, 2) as n:
                for m in range(2):
                    sp.wait_ge(drive_ready, 2 * n + (2 * m + 1))
                    sp.dma_start(b_row[:, m, :], bc_rows[bass.ds(n + (1 + m), 1), :].broadcast_to((P, T))
                                 ).then_inc(b_loaded, 16)
                    sp.wait_ge(hc_ready, 2 * n + (2 * m + 1))
                    sp.dma_start(c_row[:, m, :], bc_rows[bass.ds(n + (NS + 1 + m), 1), :].broadcast_to((P, T))
                                 ).then_inc(c_loaded, 16)
            for s in range(looped, NS):
                sp.wait_ge(b_loaded, 16 * s)
                sp.wait_ge(drive_ready, 2 * (s - 1))
                sp.dma_start(b_row[:, s % 2, :], bc_rows[s:s + 1, :].broadcast_to((P, T))).then_inc(b_loaded, 16)
                sp.wait_ge(c_loaded, 16 * s)
                sp.wait_ge(hc_ready, 2 * (s - 1))
                sp.dma_start(c_row[:, s % 2, :], bc_rows[NS + s:NS + s + 1, :].broadcast_to((P, T))).then_inc(c_loaded, 16)
            out_v = out.rearrange("b (a p) n -> b p a n", p=P)
            for b in range(B):
                sp.wait_ge(y_ready if b < B - 1 else y_last_ready, 2 * b + 2 if b < B - 1 else 2)
                sp.dma_start(out_v[b], res3[:, 2 * b:2 * b + 2, :]).then_inc(out_stored, 16)
            sp.wait_ge(out_stored, 16 * B)

        @block.tensor
        def _(pe):
            def products(o, lhs, rhs, start=True, stop=True, skip=False):
                n = len(lhs)
                for k in range(n):
                    (lh, ll), (rh, rl) = lhs[k], rhs[k]
                    pe.matmul(o, lh, rh, start=start and k == 0, stop=False, skip_group_check=skip)
                    pe.matmul(o, lh, rl, start=False, stop=False, skip_group_check=skip)
                    m = pe.matmul(o, ll, rh, start=False, stop=stop and k == n - 1, skip_group_check=skip)
                return m

            def wq(col, off):
                return [(wqkv_hi[:, k, bass.ds(col + off, D)], wqkv_lo[:, k, bass.ds(col + off, D)]) for k in range(KT)]

            def xt(at, n):
                return [(xT_hi[:, k, bass.ds(at, n)], xT_lo[:, k, bass.ds(at, n)]) for k in range(KT)]

            def q_unit(i, place, pair):
                tok, col = place
                for n in range(2):
                    m = products(ps_qkv(i, pair)[:, n * S:(n + 1) * S], wq(col, (2 * pair + n) * D), xt(tok, S))
                m.then_inc(qk_ready, 1)

            def k_unit(i, place):
                tok, col = place
                products(ps_qkv(i, 2)[:, 0:S], wq(col, QPG * D), xt(tok, S)).then_inc(qk_ready, 1)

            def v_unit(i, place):
                tok, col = place
                for t in range(2):
                    m = products(ps_qkv(i, 3)[:, t * D:(t + 1) * D], xt(tok + t * P, P), wq(col, (QPG + 1) * D))
                m.then_inc(v_ready, 1)

            def scores(i):
                pe.matmul(ps_s0, ident_b[:], mask_b[:].unsqueeze(1).broadcast_to((P, QPG, P)),
                          start=True, stop=False, skip_group_check=True)
                for h in range(QPG):
                    m = products(ps_s0[:, h, :], [(q_hi[:, h * S:h * S + P], q_lo[:, h * S:h * S + P])],
                                 [(k_hi[:, 0:P], k_lo[:, 0:P])], start=False, skip=True)
                m.then_inc(scores_ready, 1)
                for pair in range(2):
                    o = ps_s1[pair]
                    pe.matmul(o[:, :, P:S], ident_b[:], mask_b[:].unsqueeze(1).broadcast_to((P, 2, P)),
                              start=True, stop=False, skip_group_check=True)
                    for n in range(2):
                        q0 = (2 * pair + n) * S + P
                        m = products(o[:, n, :], [(q_hi[:, q0:q0 + P], q_lo[:, q0:q0 + P])], [(k_hi[:], k_lo[:])],
                                     start=False, skip=True)
                    m.then_inc(scores_ready, 1)

            def transposes(i, h):
                k = 4 * i + h
                pe.wait_ge(probs_ready, k + 1)
                if not (isinstance(k, int) and k < 2):
                    pe.wait_ge(pt_out, k - 1)
                o = ps_pt[h % 2]
                pe.transpose(o[:, 0:P], e_sb[:, h, 0:P], ident[:])
                pe.transpose(o[:, P:2 * P], e_sb[:, h, P:2 * P], ident[:])
                pe.transpose(o[:, 2 * P:3 * P], e_sb[:, h, 2 * P:3 * P], ident[:]).then_inc(pt_ready, 1)

            def pv(i, h):
                k = 4 * i + h
                pe.wait_ge(pt_out, k + 1)
                if h % 2 == 0 and not (isinstance(k, int) and k == 0):
                    pe.wait_ge(o_lo_done, 2 * i + h // 2)
                o = ps_o[:, (h % 2) * S:(h % 2 + 1) * S]
                p_t = pt_sb[:, h % 2, :]
                pe.matmul(o, v_sb[:, 0, :], p_t[:, 0:S], start=True, stop=False, skip_group_check=True)
                pe.matmul(o[:, P:S], v_sb[:, 1, :], p_t[:, S:S + P], start=False, stop=True,
                          skip_group_check=True).then_inc(pv_done, 1)

            def project(i, g, h):
                pe.wait_ge(o_lo_done, 2 * i + h // 2 + 1)
                if g == h == 0 and not (isinstance(i, int) and i == 0):
                    pe.wait_ge(proj_added, i)
                w = (wp_hi[:, g * QPG + h, :], wp_lo[:, g * QPG + h, :])
                for a in range(2):
                    m = products(ps_proj[:, a * HID:(a + 1) * HID],
                                 [(o_hi[:, h, a * P:(a + 1) * P], o_lo[:, h, a * P:(a + 1) * P])], [w],
                                 start=g == h == a == 0, stop=g == NKV - 1 and h == QPG - 1, skip=True)
                if h % 2:
                    m.then_inc(proj_done, 1)

            def x_proj(c):
                for j in range(DT):
                    m = pe.matmul(bank[5 + c][0:DTR + 2 * NS, :], xp_w[:, j, :], u[:, j, c * 512:(c + 1) * 512],
                                  start=j == 0, stop=j == DT - 1)
                m.then_inc(xp_done, 1)

            def dt_proj(j, c):
                pe.matmul(bank[5 + c][:], dt_w[:, j * P:(j + 1) * P], xdbl[0:DTR, c * 512:(c + 1) * 512],
                          start=True, stop=True).then_inc(dtp_done, 1)

            pe.wait_ge(ctx_loaded, 32)
            for j in range(DT):
                for c in range(2):
                    pe.matmul(bank[4 + 2 * j + c][:], in_w[:, j * P:(j + 1) * P], ctx_sb[:, c * 512:(c + 1) * 512],
                              start=True, stop=True).then_inc(in_done, 1)
            pe.wait_ge(x_lo_done, 1)
            pe.wait_ge(wq_lo_done, 1)
            q_unit(0, (0, 0), 0)
            pe.wait_ge(pad_done, 4)
            q_unit(0, (0, 0), 1)
            k_unit(0, (0, 0))
            v_unit(0, (0, 0))
            pe.wait_ge(qk_out, 3)
            pe.wait_ge(consts_b, 2)
            scores(0)
            pe.wait_ge(wq_lo_done, 2)
            q_unit(1, (0, GW), 0)

            def step(i, g, tok, at=lambda place: None):
                first, last = isinstance(i, int) and i == 0, isinstance(i, int) and i == NG - 1
                transposes(i, 0)
                transposes(i, 1)
                pe.wait_ge(v_out, i + 1)
                if not first:
                    project(i - 1, (g - 1) % NKV, 3)
                pv(i, 0)
                pv(i, 1)
                next_place, after_next = [(tok + (g + n) // NKV * S, (g + n) % NKV * GW) for n in (1, 2)]
                if not last:
                    pe.wait_ge(qk_out, 3 * i + 4)
                    q_unit(i + 1, next_place, 1)
                transposes(i, 2)
                transposes(i, 3)
                at("pr01")
                project(i, g, 0)
                project(i, g, 1)
                if not last:
                    pe.wait_ge(qk_out, 3 * i + 5)
                    k_unit(i + 1, next_place)
                at("pv2")
                pv(i, 2)
                pv(i, 3)
                if not last:
                    pe.wait_ge(qk_out, 3 * i + 6)
                    pe.wait_ge(exp_done, 4 * i + 4)
                    scores(i + 1)
                    at("v")
                    v_unit(i + 1, next_place)
                at("pr2")
                project(i, g, 2)
                at("q01")
                if not (isinstance(i, int) and i >= NG - 2):
                    pe.wait_ge(v_out, i + 2)
                    q_unit(i + 2, after_next, 0)
                at("end")

            def in_step0(place):
                if place == "pr01":
                    pe.wait_ge(wp_lo_done, 1)
                elif place == "pr2":
                    pe.wait_ge(pt_out, QPG)
                    pe.wait_ge(scanw_loaded, 16 * 6)
                    pe.wait_ge(u_done, 2)
                    x_proj(0)
                    x_proj(1)
                elif place == "q01":
                    pe.wait_ge(wq_lo_done, 3)
                elif place == "end":
                    pe.wait_ge(xdbl_done, 2)

            def in_step1(place):
                if place == "pr01":
                    pe.wait_ge(wp_lo_done, 2)
                elif place == "pv2":
                    pe.wait_ge(pt_out, 2 * QPG)
                    dt_proj(0, 0)
                    dt_proj(0, 1)
                elif place == "q01":
                    pe.wait_ge(wq_lo_done, NKV)
                elif place == "end":
                    pe.wait_ge(dt_out, 2)
                    pe.wait_ge(wp_lo_done, NKV)

            def in_step2(place):
                if place == "pv2":
                    pe.wait_ge(pt_out, 3 * QPG)
                    dt_proj(1, 0)
                    dt_proj(1, 1)
                elif place == "q01":
                    pe.wait_ge(x_rest_lo, 2)
                elif place == "end":
                    pe.wait_ge(dt_out, 4)

            def in_last_step(place):
                if place == "pv2":
                    add_tile(PE_TILE)
                elif place == "pr2":
                    add_tile(PE_TILE + 1)

            for i, hook in enumerate((in_step0, in_step1, in_step2)):
                step(i, i, 0, at=hook)
            with loop(PE, NKV - 1, NG - 1 - NKV, NKV) as i:
                tok = pe.alloc_register("tok")
                pe.reg_mul(tok, batch_of(i), S)
                tok = pe.snap(tok, donate=True, min_val=0, max_val=S)
                for m in range(NKV):
                    step(i + m, (m - 1) % NKV, tok + (NKV - 1 + m) // NKV * S)
            for i in range(NG - 1 - NKV, NG - 1):
                step(i, i % NKV, i // NKV * S)

            def add_tile(m):
                j = m % DT
                if m < PE_TILE + DT:
                    pe.wait_ge(exp_done, 4 * NG)
                    pe.wait_ge(v_out, NG)
                pe.wait_ge(hc_ready, m + 1)
                for c in range(2):
                    if c == 1 and m == TILES - 1:
                        pe.wait_ge(hc_last, 1)
                    a = pe.matmul(y_ps[:, 2 * j + c, :], ident[:], h_st[:, j, c * 512:(c + 1) * 512],
                                  start=m < PE_TILE + DT, stop=m >= TILES - DT)
                    if c == 1 or m == TILES - 1:
                        a.then_inc(ysum_done, 1)

            step(NG - 1, NKV - 1, (B - 1) * S, at=in_last_step)
            project(NG - 1, NKV - 1, 3)
            for m in range(PE_TILE + 2, TILES):
                add_tile(m)
                j = m - (PE_TILE + 2)
                if 0 <= j < DT:
                    pe.wait_ge(acc_done, DT + PE_TILE)
                    for c in range(2):
                        pe.matmul(y_ps[:, 2 * j + c, :], ident[:], y_acc[:, j, c * 512:(c + 1) * 512],
                                  start=False, stop=False)

            pe.wait_ge(late_loaded, 16 * 3)
            pe.wait_ge(ffn_loaded, 32)
            pe.wait_ge(proj_added, NG)

            def gated_transposes(b):
                pe.wait_ge(gated_ready, b + 1)
                for a in range(2):
                    for j in range(2):
                        m = pe.transpose(bank[4 + b][:, a * HID + j * P:a * HID + (j + 1) * P],
                                         gated[:, 2 * b + j, a * P:(a + 1) * P], ident[:])
                m.then_inc(gT_ready, 1)

            def x2_transposes(b):
                pe.wait_ge(x2_ready, 2 * b + 2)
                for k in range(KT):
                    for a in range(2):
                        m = pe.transpose(bank[4 + b][:, k * S + a * P:k * S + (a + 1) * P],
                                         res2[:, 2 * b + a, k * P:(k + 1) * P], ident[:])
                m.then_inc(x2T_ps, 1)

            def up(b):
                pe.wait_ge(x2T_ready, b + 1)
                for o in range(2):
                    for k in range(KT):
                        m = pe.matmul(bank[4 + b][:, o * S:(o + 1) * S], up_w[:, k, o * P:(o + 1) * P],
                                      x2T[:, k, b * S:(b + 1) * S], start=k == 0, stop=k == KT - 1)
                m.then_inc(up_done, 1)

            def expert_and_gate(b):
                for t in (2 * b, 2 * b + 1):
                    if t >= 4:
                        pe.wait_ge(expert_mixed, t - 3)
                    for k in range(KT):
                        m = pe.matmul(bank[t % 4][:, 0:HID + NE], x2T[:, k, t * P:(t + 1) * P], exp_w[:, k, :],
                                      start=k == 0, stop=k == KT - 1)
                    m.then_inc(expert_done, 1)

            def down(b):
                pe.wait_ge(relu_done, b + 1)
                for t in (2 * b, 2 * b + 1):
                    for k in range(KT):
                        m = pe.matmul(bank[4 + b][:, (t % 2) * HID:(t % 2 + 1) * HID], hidden[:, k, t * P:(t + 1) * P],
                                      down_w[:, k, :], start=k == 0, stop=k == KT - 1)
                m.then_inc(down_done, 1)

            for b in range(B - 1):
                gated_transposes(b)
            for b in range(B):
                x2_transposes(b)
                if b:
                    down(b - 1)
                else:
                    gated_transposes(B - 1)
                up(b)
                expert_and_gate(b)
            down(B - 1)

        @block.scalar
        def _(act):
            def pad(j, c):
                act.wait_ge(in_done, 2 * j + c + 1)
                act.activation(x_pad[:, j, 2 * c:2 * c + 2, DC - 1:],
                               bank[4 + 2 * j + c][:].rearrange("p (b l) -> p b l", b=2), ACT.Copy).then_inc(pad_done, 1)

            def wq_high(g):
                w = slice(g * GW, (g + 1) * GW)
                act.activation(wqkv_hi[:, :, w], wqkv_f[:, :, w], ACT.Copy, scale=W_SCALE).then_inc(wq_hi_done, 1)

            act.wait_ge(x_loaded, 16)
            act.activation(xT_hi[:, :, 0:S], xT_f[:, :, 0:S], ACT.Copy).then_inc(x_hi_done, 1)
            pad(0, 0)
            pad(0, 1)
            act.wait_ge(wq0_loaded, 16)
            wq_high(0)
            pad(1, 0)
            pad(1, 1)
            act.wait_ge(wq1_loaded, 16)
            wq_high(1)

            def qk_high(i, unit):
                act.wait_ge(qk_ready, 3 * i + unit + 1)
                o, n = ((q_hi[:, 0:512], 512), (q_hi[:, 512:1024], 512), (k_hi[:], 256))[unit]
                act.activation(o, ps_qkv(i, unit)[:, 0:n], ACT.Copy, scale=QK_OUT).then_inc(qk_hi, 1)

            def exps(i):
                for h in range(QPG):
                    top_exp(i, h)
                v_copy(i)
                for h in range(QPG):
                    bottom_exp(i, h)

            def top_exp(i, h):
                act.wait_ge(max_done, 3 * i + 1)
                if not (isinstance(i, int) and i == 0):
                    act.wait_ge(pt_ready, 4 * i + h - 3)
                act.activation(e_sb[:, h, 0:P], ps_s0[:, h, :], ACT.Exp, bias=negmax[:, h:h + 1], accum_out=esum[:, h, 0:1])

            def bottom_exp(i, h):
                act.wait_ge(max_done, 3 * i + 2 + h // 2)
                act.activation(e_sb[:, h, P:], ps_s1[h // 2][:, h % 2, :], ACT.Exp, bias=negmax[:, QPG + h:QPG + h + 1],
                               accum_out=esum[:, h, 1:2]).then_inc(exp_done, 1)

            def v_copy(i):
                act.wait_ge(v_ready, i + 1)
                act.activation(v_sb[:].rearrange("p t d -> p (t d)"), ps_qkv(i, 3)[:, 0:2 * D], ACT.Copy,
                               scale=V_OUT).then_inc(v_out, 1)

            def pt_copy(i, h):
                k = 4 * i + h
                act.wait_ge(pt_ready, k + 1)
                if not (isinstance(k, int) and k < 2):
                    act.wait_ge(pv_done, k - 1)
                act.activation(pt_sb[:, h % 2, :], ps_pt[h % 2][:, 0:3 * P], ACT.Copy).then_inc(pt_out, 1)

            def o_high(i, pair):
                act.wait_ge(pv_done, 4 * i + 2 * pair + 2)
                if not (isinstance(i, int) and i == 0):
                    act.wait_ge(proj_done, 2 * i + pair - 1)
                act.activation(o_hi[:, 2 * pair:2 * pair + 2, :].rearrange("p h s -> p (h s)"), ps_o[:],
                               ACT.Copy).then_inc(o_hi_done, 1)

            def scan_decay(n, j):
                if isinstance(n, int) and n == 0:
                    act.wait_ge(zero_done, j + 1)
                else:
                    act.wait_ge(scan_done, 2 * n + (j - 1))
                act.activation(decay[:, j, :].rearrange("p (b l) -> p b l", b=B)[:, :, 1:],
                               dt[:, j, :].rearrange("p (b l) -> p b l", b=B)[:, :, 1:], ACT.Exp,
                               scale=a_mat[:, j, bass.ds(n, 1)]).then_inc(decay_ready, 1)

            for unit in range(3):
                qk_high(0, unit)
            act.wait_ge(wp0_loaded, 16)
            act.activation(wp_hi[:, 0:QPG, :], wp_f[:, 0:QPG, :], ACT.Copy, scale=W_SCALE).then_inc(wp_hi_done, 1)
            exps(0)

            def step(i, slot, last=False):
                if not last:
                    qk_high(i + 1, 0)
                pt_copy(i, 0)
                pt_copy(i, 1)
                slot("q01")
                o_high(i, 0)
                slot("q23")
                if not last:
                    qk_high(i + 1, 1)
                pt_copy(i, 2)
                pt_copy(i, 3)
                slot("k")
                if not last:
                    qk_high(i + 1, 2)
                slot("o")
                o_high(i, 1)
                slot("exps")
                if not last:
                    exps(i + 1)
                slot("end")

            def in_step0(slot):
                if slot == "k":
                    act.wait_ge(scanw_loaded, 16 * 6)
                    act.activation(a_mat[:], a_mat[:], ACT.Exp).then_inc(a_exp, 1)
                    act.preload_act_table(ACT.Silu)
                if slot == "exps":
                    act.wait_ge(conv0_done, DC)
                    act.activation(u[:, 0, :], decay[:, 0, :], ACT.Silu, bias=cb[:, 0:1]).then_inc(u_done, 1)
                    act.wait_ge(conv1_done, 2 * DC - 1)
                    act.activation(u[:, 1, :], decay[:, 1, :], ACT.Silu, bias=cb[:, 1:2]).then_inc(u_done, 1)
                if slot == "end":
                    for c in range(2):
                        act.wait_ge(xp_done, c + 1)
                        act.activation(xdbl[:, c * 512:(c + 1) * 512], bank[5 + c][0:DTR + 2 * NS, :],
                                       ACT.Copy).then_inc(xdbl_done, 1)

            def dt_copy(j, c):
                act.wait_ge(dtp_done, 2 * j + c + 1)
                w = slice(c * 512, (c + 1) * 512)
                act.activation(decay[:, j, w], bank[5 + c][:], ACT.Abs, bias=dtb[:, j:j + 1])
                act.activation(du[:, j, w], bank[5 + c][:], ACT.Relu, bias=dtb[:, j:j + 1]).then_inc(dt_out, 1)

            def soft_exp(j):
                act.wait_ge(dt_out, 2 * j + 2)
                act.activation(decay[:, j, :], decay[:, j, :], ACT.Exp, scale=-1.0).then_inc(sp_exp, 1)

            def soft_log(j):
                act.wait_ge(sp_exp, j + 1)
                act.activation(dt[:, j, :], decay[:, j, :], ACT.Ln, bias=1.0).then_inc(sp_ln, 1)

            def in_step1(slot):
                if slot == "k":
                    act.wait_ge(x_rest_loaded, 16)
                    act.activation(xT_hi[:, :, S:], xT_f[:, :, S:], ACT.Copy).then_inc(x_hi_done, 1)
                if slot == "o":
                    dt_copy(0, 0)
                    dt_copy(0, 1)

            def in_step2(slot):
                if slot == "q01":
                    soft_exp(0)
                if slot == "k":
                    soft_log(0)
                    act.preload_act_table(ACT.Exp)
                if slot == "o":
                    dt_copy(1, 0)
                    dt_copy(1, 1)

            def in_step3(slot):
                if slot == "q01":
                    soft_exp(1)
                if slot == "q23":
                    act.wait_ge(a_done, 1)
                    act.wait_ge(dt_ready, 1)
                    scan_decay(0, 0)
                if slot == "k":
                    act.preload_act_table(ACT.Ln)
                if slot == "o":
                    soft_log(1)
                if slot == "exps":
                    act.preload_act_table(ACT.Exp)

            def in_step4(slot):
                if slot == "q01":
                    act.wait_ge(dt_ready, 2)
                    scan_decay(0, 1)
                if slot == "q23":
                    scan_decay(1, 0)
                if slot == "k":
                    scan_decay(1, 1)

            def scan_slots(n):
                places = {"q01": 0, "k": 1}
                return lambda slot: scan_decay(n, places[slot]) if slot in places else None

            step(0, in_step0)
            step(1, in_step1)
            step(2, in_step2)
            step(LAG, in_step3)
            step(LAG + 1, in_step4)
            with loop(ACTE, LAG + 2, NG - 1) as i:
                step(i, scan_slots(i - LAG))

            def in_last_step(slot):
                scan_slots(NG - 1 - LAG)(slot)
                if slot == "o":
                    scan_decay(NG - LAG, 0)

            step(NG - 1, in_last_step, last=True)

            def x1(b):
                act.wait_ge(shift_done, b + 1)
                for t in (2 * b, 2 * b + 1):
                    act.activation(resid[:, t, :], resid[:, t, :], ACT.Identity, bias=shift[:, t:t + 1],
                                   scale=rstd[:, t:t + 1]).then_inc(x1_ready, 1)

            for n in range(NG - LAG, NS):
                for j in range(1 if n == NG - LAG else 0, DT):
                    scan_decay(n, j)
                if n == NG - LAG:
                    x1(0)
                    x1(1)
                elif n == NS - 2:
                    x1(2)
                    x1(3)

            for b in range(B):
                act.wait_ge(x1_ready, 2 * b + 2)
                act.activation(z_silu[:, 2 * b:2 * b + 2, :], resid[:, 2 * b:2 * b + 2, :], ACT.Silu).then_inc(z_ready, 1)
            act.preload_act_table(ACT.Exp)

            def x2T_copy(b):
                act.wait_ge(x2T_ps, b + 1)
                act.activation(x2T[:, :, b * S:(b + 1) * S], bank[4 + b].rearrange("p (k s) -> p k s", k=KT),
                               ACT.Copy).then_inc(x2T_ready, 1)

            def relu(b):
                act.wait_ge(up_done, b + 1)
                act.activation(hidden[:, :, b * S:(b + 1) * S], bank[4 + b].rearrange("p (k s) -> p k s", k=KT),
                               ACT.Relu).then_inc(relu_done, 1)

            def route_exps(b):
                act.wait_ge(route, 7 * b + 3)
                act.activation(top_e[:, 2 * b:2 * b + 2, :], top_d[:, 2 * b:2 * b + 2, :], ACT.Exp).then_inc(route_exp, 1)

            def last_norm(b):
                act.wait_ge(shift_done, B + b + 1)
                for t in (2 * b, 2 * b + 1):
                    act.activation(res3[:, t, :], res3[:, t, :], ACT.Identity, bias=shift[:, t:t + 1],
                                   scale=rstd[:, t:t + 1]).then_inc(y_ready, 1)

            for b in range(B):
                x2T_copy(b)
                if b:
                    route_exps(b - 1)
                relu(b)
            last_norm(0)
            route_exps(B - 1)
            last_norm(1)
            last_norm(2)

        @block.vector
        def _(dve):
            dve.wait_ge(x_hi_done, 1)
            dve.tensor_tensor(xT_lo[:, :, 0:S], xT_f[:, :, 0:S], xT_hi[:, :, 0:S], ALU.subtract).then_inc(x_lo_done, 1)

            def wq_low(g):
                dve.wait_ge(wq_hi_done, g + 1)
                w = slice(g * GW, (g + 1) * GW)
                dve.scalar_tensor_tensor(out=wqkv_lo[:, :, w], in0=wqkv_f[:, :, w], scalar=W_SCALE, in1=wqkv_hi[:, :, w],
                                         op0=ALU.mult, op1=ALU.subtract).then_inc(wq_lo_done, 1)

            def wp_low(g):
                dve.wait_ge(wp_hi_done, g + 1)
                w = slice(g * QPG, (g + 1) * QPG)
                dve.scalar_tensor_tensor(out=wp_lo[:, w, :], in0=wp_f[:, w, :], scalar=W_SCALE, in1=wp_hi[:, w, :],
                                         op0=ALU.mult, op1=ALU.subtract).then_inc(wp_lo_done, 1)

            def conv_tap(k):
                acc = decay[:, 0, :].rearrange("p (b l) -> p b l", b=B)
                if k == 0:
                    dve.wait_ge(cw_loaded, 16)
                    dve.wait_ge(pad_zeroed, 1)
                    dve.wait_ge(pad_done, 2)
                    dve.tensor_scalar(acc, x_pad[:, 0, :, 0:S], cw[:, 0, 0:1], None, ALU.mult).then_inc(conv0_done, 1)
                else:
                    dve.wait_ge(conv0_done, k)
                    dve.scalar_tensor_tensor(out=acc, in0=x_pad[:, 0, :, k:k + S], scalar=cw[:, 0, k:k + 1], in1=acc,
                                             op0=ALU.mult, op1=ALU.add).then_inc(conv0_done, 1)

            def qkv_low(i, unit):
                dve.wait_ge(qk_hi, 3 * i + unit + 1)
                o, hi, n = ((q_lo[:, 0:512], q_hi[:, 0:512], 512), (q_lo[:, 512:1024], q_hi[:, 512:1024], 512),
                            (k_lo[:], k_hi[:], 256))[unit]
                dve.scalar_tensor_tensor(out=o, in0=ps_qkv(i, unit)[:, 0:n], scalar=QK_OUT, in1=hi, op0=ALU.mult,
                                         op1=ALU.subtract).then_inc(qk_out, 1)

            def row_max(i, n):
                o, ps = ((negmax[:, 0:QPG], ps_s0), (negmax[:, QPG:QPG + 2], ps_s1[0]), (negmax[:, QPG + 2:], ps_s1[1]))[n]
                dve.wait_ge(scores_ready, 3 * i + n + 1)
                dve.tensor_reduce(o, ps, AX.X, ALU.max, negate=True).then_inc(max_done, 1)

            def normalise_probs(i, h):
                dve.wait_ge(exp_done, 4 * i + h + 1)
                dve.reciprocal(rsum[:, h, :], esum[:, h, :]).then_inc(rsum_ready, 1)
                dve.wait_ge(rsum_ready, 4 * i + h + 1)
                dve.tensor_scalar(e_sb[:, h, 0:P], e_sb[:, h, 0:P], rsum[:, h, 0:1], None, ALU.mult)
                dve.tensor_scalar(e_sb[:, h, P:], e_sb[:, h, P:], rsum[:, h, 1:2], None, ALU.mult).then_inc(probs_ready, 1)

            def add_projection(i):
                dve.wait_ge(proj_done, 2 * i + 2)
                dve.wait_ge(late_loaded, 16 * 3)
                r = resid[:, bass.ds(batch_of(i) * 2, 2), :].rearrange("p a n -> p (a n)")
                dve.scalar_tensor_tensor(out=r, in0=ps_proj[:], scalar=Y_OUT, in1=r, op0=ALU.mult,
                                         op1=ALU.add).then_inc(proj_added, NKV)

            def o_low(i, pair):
                dve.wait_ge(o_hi_done, 2 * i + pair + 1)
                dve.tensor_tensor(o_lo[:, 2 * pair:2 * pair + 2, :].rearrange("p h s -> p (h s)"), ps_o[:],
                                  o_hi[:, 2 * pair:2 * pair + 2, :].rearrange("p h s -> p (h s)"),
                                  ALU.subtract).then_inc(o_lo_done, 1)

            def scan(n, j):
                m = 2 * n + j
                dve.wait_ge(decay_ready, m + 1)
                dve.wait_ge(drive_ready, m + 1)
                if isinstance(m, int) and m >= PE_TILE + DT:
                    dve.wait_ge(ysum_done, m - DT - PE_TILE + 1)
                else:
                    dve.wait_ge(acc_done, m + 1)
                dve.tensor_tensor_scan(h_st[:, j, 0:T], decay[:, j, :], drive[:, j, :], 0.0, ALU.mult,
                                       ALU.add).then_inc(scan_done, 1)

            def times_c(n, j, half=None):
                if half is None:
                    half = n % 2
                dve.wait_ge(scan_done, 2 * n + j + 1)
                dve.wait_ge(c_loaded, 16 * n + 16)
                dve.tensor_tensor(h_st[:, j, 0:T], h_st[:, j, 0:T], c_row[:, half, :],
                                  ALU.mult).then_inc(hc_ready, 1)

            conv_tap(0)
            wq_low(0)
            conv_tap(1)
            wq_low(1)
            qkv_low(0, 0)
            qkv_low(0, 1)
            qkv_low(0, 2)
            for n in range(3):
                row_max(0, n)
            normalise_probs(0, 0)
            normalise_probs(0, 1)

            def step(i, slot, adds=False, last=False):
                normalise_probs(i, 2)
                normalise_probs(i, 3)
                if not last:
                    qkv_low(i + 1, 0)
                slot(0)
                if adds:
                    add_projection(i - 1)
                o_low(i, 0)
                slot(1)
                if not last:
                    qkv_low(i + 1, 1)
                slot(2)
                if not last:
                    qkv_low(i + 1, 2)
                slot(3)
                slot(4)
                if not last:
                    row_max(i + 1, 0)
                o_low(i, 1)
                if not last:
                    row_max(i + 1, 1)
                    row_max(i + 1, 2)
                slot(5)
                if not last:
                    normalise_probs(i + 1, 0)
                    normalise_probs(i + 1, 1)
                slot(6)

            def series_of_tile1(op):
                e, r = decay[:, 1, :], drive[:, 1, :]
                if op == 0:
                    dve.wait_ge(sp_exp, 2)
                    dve.tensor_scalar(r, e, 1.0 / 3.0, -0.5, ALU.mult, ALU.add).then_inc(series1, 1)
                elif op == 1:
                    dve.wait_ge(series1, 1)
                    dve.tensor_tensor(r, r, e, ALU.mult).then_inc(series1, 1)
                else:
                    dve.wait_ge(series1, 2)
                    dve.scalar_tensor_tensor(out=r, in0=r, scalar=1.0, in1=e, op0=ALU.add, op1=ALU.mult).then_inc(series1, 1)

            def small_of(j):
                dve.wait_ge(sp_exp, j + 1)
                dve.tensor_scalar(h_st[:, j, 0:T], decay[:, j, :], SMALL, None, ALU.is_lt).then_inc(dt_small, 1)

            def log1p_of(j):
                dve.wait_ge(dt_small, j + 1)
                dve.wait_ge(series1 if j else series0, 3 if j else 4)
                dve.wait_ge(sp_ln, j + 1)
                dve.copy_predicated(dt[:, j, :], h_st[:, j, 0:T].bitcast(I32), drive[:, j, :]).then_inc(dt_log, 1)
                dve.memset(decay[:, j, :].rearrange("p (b l) -> p b l", b=B)[:, :, 0:1], 0.0).then_inc(zero_done, 1)

            def in_step0(slot):
                if slot == 0:
                    wp_low(0)
                if slot == 1:
                    conv_tap(2)
                if slot == 2:
                    conv_tap(3)
                if slot == 3:
                    wq_low(2)
                    dve.wait_ge(a_exp, 1)
                    dve.tensor_scalar(a_mat[:], a_mat[:], -1.0, None, ALU.mult).then_inc(a_done, 1)
                if slot == 5:
                    wp_low(1)

            def in_step1(slot):
                if slot == 0:
                    wq_low(3)
                if slot == 1:
                    wp_low(2)
                if slot == 2:
                    wp_low(3)

            def in_step2(slot):
                if slot == 1:
                    small_of(0)
                if slot == 4:
                    log1p_of(0)

            def in_step3(slot):
                if slot == 0:
                    series_of_tile1(0)
                    series_of_tile1(1)
                if slot == 2:
                    series_of_tile1(2)
                    small_of(1)
                if slot == 3:
                    scan(0, 0)
                if slot == 6:
                    times_c(0, 0)
                if slot == 4:
                    log1p_of(1)

            def scan_slots(n, half=None):
                if half is None:
                    half = n % 2

                def slot(s):
                    if s < 2 and isinstance(n, int) and n == 0:
                        return
                    if s == 0:
                        scan(n - 1, 1)
                    elif s == 1:
                        times_c(n - 1, 1, 1 - half)
                    elif s == 2:
                        scan(n, 0)
                    elif s == 3:
                        times_c(n, 0, half)
                return slot

            step(0, in_step0)
            step(1, in_step1)
            step(2, in_step2)
            step(LAG, in_step3)
            with loop(DVE, LAG + 1, NG - NKV, NKV) as i:
                for m in range(NKV):
                    step(i + m, scan_slots(i + (m - LAG), (m + 1) % 2), adds=m == 0)
            def tile_stats(buf, t):
                dve.bn_stats(stats[:, t, :], buf[:, t, :]).then_inc(st_done, 1)

            def batch_moments(buf, nth, b):
                tile_stats(buf, 2 * b)
                tile_stats(buf, 2 * b + 1)
                batch_aggregate(nth, b)

            def batch_aggregate(nth, b):
                n, two = B * nth + b, slice(2 * b, 2 * b + 2)
                dve.wait_ge(st_done, 2 * n + 2)
                for t in (2 * b, 2 * b + 1):
                    dve.bn_aggr(mv[:, t, :], stats[:, t, :]).then_inc(mv_done, 1)
                dve.wait_ge(mv_done, 2 * n + 2)
                dve.tensor_scalar(veps[:, two], mv[:, two, 1], EPS, None, ALU.add).then_inc(veps_done, 1)

            def moments_slots(i):
                b = i - (NG - NKV)

                def slot(s):
                    scan_slots(i - LAG)(s)
                    if s == 0:
                        dve.wait_ge(proj_added, NKV * (b + 1))
                        tile_stats(resid, 2 * b)
                    elif s == 2:
                        tile_stats(resid, 2 * b + 1)
                    elif s == 4:
                        batch_aggregate(0, b)
                return slot

            for i in range(NG - NKV, NG - 1):
                step(i, moments_slots(i), adds=i == NG - NKV)

            def mean_shift(nth, b):
                two = slice(2 * b, 2 * b + 2)
                dve.wait_ge(rstd_done, B * nth + b + 1)
                dve.scalar_tensor_tensor(out=shift[:, two], in0=mv[:, two, 0], scalar=-1.0, in1=rstd[:, two],
                                         op0=ALU.mult, op1=ALU.mult).then_inc(shift_done, 1)

            def normalise(buf, nth, b, done):
                dve.wait_ge(rstd_done, B * nth + b + 1)
                for t in (2 * b, 2 * b + 1):
                    dve.tensor_scalar(buf[:, t, :], buf[:, t, :], mv[:, t, 0:1], rstd[:, t:t + 1], ALU.subtract,
                                      ALU.mult).then_inc(done, 1)

            def in_last_step(slot):
                scan_slots(NG - 1 - LAG)(slot)
                if slot == 4:
                    scan(NG - 1 - LAG, 1)

            step(NG - 1, in_last_step, last=True)
            for m in range(PE_TILE + 2, TILES - 1):
                n, j = divmod(m, DT)
                if m > PE_TILE + 2:
                    scan(n, j)
                times_c(n, j)
                if m == PE_TILE + 2:
                    for b in range(B - 1):
                        mean_shift(0, b)
                elif m == PE_TILE + 3:
                    add_projection(NG - 1)
                    dve.wait_ge(proj_added, NG)
                    batch_moments(resid, 0, B - 1)
                elif m == PE_TILE + 4:
                    mean_shift(0, B - 1)

            dve.wait_ge(decay_ready, TILES)
            dve.wait_ge(drive_ready, TILES)
            dve.wait_ge(ysum_done, TILES - 1 - DT - PE_TILE + 1)
            dve.wait_ge(c_loaded, 16 * NS)
            for c in range(2):
                w = slice(c * 512, (c + 1) * 512)
                h = h_st[:, DT - 1, w]
                dve.tensor_tensor_scan(h, decay[:, DT - 1, w], drive[:, DT - 1, w], 0.0, ALU.mult,
                                       ALU.add).then_inc(scan_done, 1)
                dve.wait_ge(scan_done, TILES + c)
                dve.tensor_tensor(h, h, c_row[:, (NS - 1) % 2, w], ALU.mult).then_inc(hc_last if c else hc_ready, 1)

            gate_in = y_ps[:].rearrange("p (j c) (b l) -> p (c b) j l", j=DT, b=2)

            def gate(b):
                dve.wait_ge(z_ready, b + 1)
                dve.wait_ge(ysum_done, TILES - PE_TILE + b // 2)
                dve.tensor_tensor(gated[:, 2 * b:2 * b + 2, :], gate_in[:, b, :, :], z_silu[:, 2 * b:2 * b + 2, :],
                                  ALU.mult).then_inc(gated_ready, 1)

            def second_residual(b):
                dve.wait_ge(x1_ready, 2 * b + 2)
                dve.wait_ge(gT_ready, b + 1)
                dve.tensor_tensor(res2[:, 2 * b:2 * b + 2, :], bank[4 + b].rearrange("p (a n) -> p a n", a=2),
                                  resid[:, 2 * b:2 * b + 2, :], ALU.add).then_inc(res2_ready, 1)

            def gates(b):
                two = slice(2 * b, 2 * b + 2)
                for t in (2 * b, 2 * b + 1):
                    dve.wait_ge(expert_done, t + 1)
                    dve.max(top[:, t, :], bank[t % 4][:, HID:HID + NE]).then_inc(route, 1)
                dve.wait_ge(route, 7 * b + 2)
                dve.tensor_tensor(top_d[:, two, :], top[:, two, 0:2], top[:, two, 0:1].broadcast_to((P, 2, 2)),
                                  ALU.subtract).then_inc(route, 1)

            def routing_weights(b):
                n, two = 7 * b, slice(2 * b, 2 * b + 2)
                dve.wait_ge(route_exp, b + 1)
                dve.tensor_tensor(top_s[:, two, :], top_e[:, two, 0:1], top_e[:, two, 1:2], ALU.add).then_inc(route, 1)
                dve.wait_ge(route, n + 4)
                dve.reciprocal(top_r[:, two, :], top_s[:, two, :]).then_inc(route, 1)
                dve.wait_ge(route, n + 5)
                dve.tensor_tensor(rw[:, two, :], top_e[:, two, :], top_r[:, two, :].broadcast_to((P, 2, 2)),
                                  ALU.mult).then_inc(route, 1)
                dve.wait_ge(route, n + 6)
                dve.tensor_tensor(rw_sum[:, two, :], rw[:, two, 0:1], rw[:, two, 1:2], ALU.add).then_inc(route, 1)

            def mix_expert(b):
                dve.wait_ge(route, 7 * b + 7)
                dve.wait_ge(x2_ready, 2 * b + 2)
                for t in (2 * b, 2 * b + 1):
                    dve.scalar_tensor_tensor(out=res3[:, t, :], in0=bank[t % 4][:, 0:HID], scalar=rw_sum[:, t, :],
                                             in1=res2[:, t, :], op0=ALU.mult, op1=ALU.add).then_inc(expert_mixed, 1)

            def mix_shared(b):
                dve.wait_ge(down_done, b + 1)
                dve.wait_ge(expert_mixed, 2 * b + 2)
                r = res3[:, 2 * b:2 * b + 2, :].rearrange("p a n -> p (a n)")
                dve.tensor_tensor(r, bank[4 + b], r, ALU.add).then_inc(shared_mixed, 1)

            def last_moments(b):
                dve.wait_ge(shared_mixed, b + 1)
                batch_moments(res3, 2, b)

            gate(0)
            gate(1)
            second_residual(0)
            for b in range(B):
                dve.wait_ge(res2_ready, b + 1)
                batch_moments(res2, 1, b)
                if b == 0:
                    gate(2)
                elif b < B - 1:
                    second_residual(b + 1)
                normalise(res2, 1, b, x2_ready)
                if b == 0:
                    gate(3)
                    second_residual(1)
                if b == B - 1:
                    last_moments(0)
                if b:
                    gates(b - 1)
                    if b > 1:
                        mix_shared(b - 2)
                    if b == B - 1:
                        mean_shift(2, 0)
                    routing_weights(b - 1)
                    mix_expert(b - 1)
            last_moments(1)
            mix_shared(2)
            gates(3)
            mean_shift(2, 1)
            last_moments(2)
            routing_weights(3)
            mix_expert(3)
            mean_shift(2, 2)
            mix_shared(3)
            last_moments(3)
            normalise(res3, 2, 3, y_last_ready)

        @block.gpsimd
        def _(pool):
            pool.memset(x_pad[:, :, :, 0:DC - 1], 0.0).then_inc(pad_zeroed, 1)
            pool.memset(mask_f[:], 0.0).then_inc(consts, 1)
            pool.memset(mhalf[:], -0.5)
            pool.memset(ident[:], 0.0).then_inc(consts, 1)
            pool.wait_ge(consts, 2)
            pool.affine_select(out=ident[:], in_=ident[:], compare_op=ALU.not_equal, fill=1.0, base=0, pattern=[[-1, P]],
                               channel_multiplier=1).then_inc(consts, 1)
            pool.affine_select(out=mask_f[:], in_=mask_f[:], compare_op=ALU.is_ge, fill=MASKED, base=0, pattern=[[-1, P]],
                               channel_multiplier=1).then_inc(consts, 1)
            pool.wait_ge(consts, 4)
            pool.tensor_copy(ident_b[:], ident[:]).then_inc(consts_b, 1)
            pool.tensor_copy(mask_b[:], mask_f[:]).then_inc(consts_b, 1)

            def wq_high(g):
                w = slice(g * GW, (g + 1) * GW)
                pool.tensor_scalar(wqkv_hi[:, :, w], wqkv_f[:, :, w], W_SCALE, 1.0, ALU.mult, ALU.mult).then_inc(wq_hi_done, 1)

            def wp_high(g):
                w = slice(g * QPG, (g + 1) * QPG)
                pool.tensor_scalar(wp_hi[:, w, :], wp_f[:, w, :], W_SCALE, 1.0, ALU.mult, ALU.mult).then_inc(wp_hi_done, 1)

            def conv_tap(k):
                acc = decay[:, 1, :].rearrange("p (b l) -> p b l", b=B)
                tap = drive[:, 1, :].rearrange("p (b l) -> p b l", b=B)
                if k == 0:
                    pool.wait_ge(pad_done, 4)
                else:
                    pool.wait_ge(conv1_done, 2 * k - 1)
                pool.tensor_scalar(acc if k == 0 else tap, x_pad[:, 1, :, k:k + S], cw[:, 1, k:k + 1], 1.0, ALU.mult,
                                   ALU.mult).then_inc(conv1_done, 1)
                if k:
                    pool.wait_ge(conv1_done, 2 * k)
                    pool.tensor_tensor(acc, acc, tap, ALU.add).then_inc(conv1_done, 1)

            pool.wait_ge(cw_loaded, 16)
            for k in range(DC):
                conv_tap(k)
            pool.wait_ge(wq_loaded, 16)
            pool.wait_ge(wq_hi_done, 2)
            wq_high(2)
            pool.wait_ge(wp_loaded, 16)
            pool.wait_ge(wp_hi_done, 1)
            wp_high(1)
            wq_high(3)
            wp_high(2)
            wp_high(3)
            pool.wait_ge(x_hi_done, 2)
            for k in range(KT):
                pool.tensor_tensor(xT_lo[:, k, S:], xT_f[:, k, S:], xT_hi[:, k, S:], ALU.subtract).then_inc(x_rest_lo, 1)
            pool.wait_ge(scanw_loaded, 16 * 6)
            for j in range(DT):
                pool.wait_ge(u_done, j + 1)
                pool.tensor_scalar(y_acc[:, j, :], u[:, j, :], d_col[:, j:j + 1], 1.0, ALU.mult, ALU.mult).then_inc(acc_done, 1)

            def softplus(j):
                pool.wait_ge(dt_log, j + 1)
                pool.tensor_tensor(dt[:, j, :], dt[:, j, :], du[:, j, :], ALU.add).then_inc(dt_ready, 1)

            def dt_u(j):
                pool.wait_ge(dt_ready, j + 1)
                pool.tensor_tensor(du[:, j, :], dt[:, j, :], u[:, j, :], ALU.mult).then_inc(du_done, 1)

            def drive_in(n, j, half):
                pool.wait_ge(b_loaded, 16 * n + 16)
                if isinstance(n, int) and n == 0:
                    pool.wait_ge(zero_done, j + 1)
                else:
                    pool.wait_ge(scan_done, 2 * n + (j - 1))
                pool.tensor_tensor(drive[:, j, :], du[:, j, :], b_row[:, half, :], ALU.mult).then_inc(drive_ready, 1)

            def accumulate(n, j):
                pool.wait_ge(hc_ready, 2 * n + j + 1)
                pool.wait_ge(acc_done, 2 * n + j + 1)
                pool.tensor_tensor(y_acc[:, j, :], y_acc[:, j, :], h_st[:, j, 0:T], ALU.add).then_inc(acc_done, 1)

            e, r = decay[:, 0, :], drive[:, 0, :]
            pool.wait_ge(sp_exp, 1)
            pool.tensor_scalar(r, e, 1.0 / 3.0, -0.5, ALU.mult, ALU.add).then_inc(series0, 1)
            pool.wait_ge(series0, 1)
            pool.tensor_tensor(r, r, e, ALU.mult).then_inc(series0, 1)
            pool.wait_ge(series0, 2)
            pool.tensor_scalar(r, r, 1.0, 1.0, ALU.mult, ALU.add).then_inc(series0, 1)
            pool.wait_ge(series0, 3)
            pool.tensor_tensor(r, r, e, ALU.mult).then_inc(series0, 1)
            softplus(0)
            dt_u(0)
            pool.wait_ge(du_done, 1)
            drive_in(0, 0, 0)
            softplus(1)
            dt_u(1)
            pool.wait_ge(du_done, 2)
            drive_in(0, 1, 0)

            def inverse_std(nth, b):
                n, two = B * nth + b, slice(2 * b, 2 * b + 2)
                pool.wait_ge(veps_done, n + 1)
                pool.tensor_tensor(rstd[:, two], veps[:, two], mhalf[:, two], ALU.pow).then_inc(rstd_done, 1)

            last = PE_TILE // DT
            with loop(POOL, 0, last // 2 * 2, 2) as n:
                for m in range(2):
                    for j in range(DT):
                        accumulate(n + m, j)
                        drive_in(n + m + 1, j, (m + 1) % 2)
            for n in range(last // 2 * 2, last):
                for j in range(DT):
                    accumulate(n, j)
                    drive_in(n + 1, j, (n + 1) % 2)
            accumulate(last, 0)
            for b in range(B - 1):
                inverse_std(0, b)
            for n in range(last, NS - 1):
                for j in range(DT):
                    if DT * (n + 1) + j == PE_TILE + 6:
                        inverse_std(0, B - 1)
                    drive_in(n + 1, j, (n + 1) % 2)
            for b in range(B, 3 * B):
                inverse_std(*divmod(b, B))


def kernel(x, ctx_1024, L0_attn_weight_qkv, L0_attn_weight_proj, L0_xattn_in_proj_w, L0_xattn_conv_w, L0_xattn_conv_b,
           L0_xattn_x_proj_w, L0_xattn_dt_proj_w, L0_xattn_dt_proj_b, L0_xattn_A_log, L0_xattn_D, L0_ffn_W_up, L0_ffn_W_down,
           L0_ffn_W_gate, L0_ffn_W_expert):
    import numpy as np
    import concourse.bacc as bacc
    from concourse.bass_utils import run_bass_kernel_spmd

    x2 = np.asarray(x).reshape(B * S, HID)
    layout = {
        "xT": x2.T, "x": x2, "wqkvT": np.asarray(L0_attn_weight_qkv).T, "wpT": np.asarray(L0_attn_weight_proj).T,
        "ctxT": np.asarray(ctx_1024).reshape(B * S, DM).T, "inT": np.asarray(L0_xattn_in_proj_w).T,
        "conv_w": np.asarray(L0_xattn_conv_w).reshape(2 * P, DC), "conv_b": L0_xattn_conv_b,
        "xprojT": np.asarray(L0_xattn_x_proj_w).T, "dtT": np.asarray(L0_xattn_dt_proj_w).T, "dt_b": L0_xattn_dt_proj_b,
        "A_log": L0_xattn_A_log, "D_skip": L0_xattn_D, "upT": np.asarray(L0_ffn_W_up).T, "downT": np.asarray(L0_ffn_W_down).T,
        "gateT": np.asarray(L0_ffn_W_gate).T, "expert": L0_ffn_W_expert,
    }
    nc = bacc.Bacc("TRN2", target_bir_lowering=False, num_devices=1)
    arrays, args = {}, []
    for name, a in layout.items():
        a = np.ascontiguousarray(a)
        arrays[f"in_{name}"] = a
        args.append(nc.dram_tensor(f"in_{name}", a.shape, mybir.dt.from_np(a.dtype), kind="ExternalInput").ap())
    args.append(nc.dram_tensor("out_y", (B, S, HID), F32, kind="ExternalOutput").ap())
    decoder_kernel(nc, *args)
    r = run_bass_kernel_spmd(nc, [arrays], core_ids=[0])
    return r.results[0]["out_y"]
```
